# Optimizing a Trainium2 kernel written in Bass

```python
import numpy as np
import jax
import jax.numpy as jnp

def _softmax(x, axis=-1):
    return jax.nn.softmax(x, axis=axis)

def _gelu(x):
    return jax.nn.gelu(x, approximate=True)

def _silu(x):
    return jax.nn.silu(x)

def _sigmoid(x):
    return jax.nn.sigmoid(x)

def _layernorm(x, axis=-1, eps=1e-05):
    m = jnp.mean(x, axis=axis, keepdims=True)
    v = jnp.var(x, axis=axis, keepdims=True)
    return (x - m) / jnp.sqrt(v + eps)

def _scatter_add(tgt, idx, src, axis=0):
    return tgt.at[idx].add(src)

def _segment_sum(src, seg, n):
    return jax.ops.segment_sum(src, seg, n)
kernel_name = 'mk_gnn_preln_d2_gnn_r16_6687ea'

def setup_inputs(seed: int=0):
    np.random.seed(seed)
    _w = jnp.asarray

    def _rec_inputs():
        import jax
        import jax.numpy as jnp
        _gk = jax.random.key(seed)
        x = -0.000202 + 1 * jax.random.normal(jax.random.fold_in(_gk, 1), (6250, 128), jnp.float32)
        _s = jax.random.randint(jax.random.fold_in(_gk, 2), (50000,), 0, 6250, jnp.int32)
        _d = jax.random.randint(jax.random.fold_in(_gk, 3), (50000,), 0, 6250, jnp.int32)
        _loop = jnp.arange(6250, dtype=jnp.int32)
        src = jnp.concatenate([_s, _d, _loop])
        dst = jnp.concatenate([_d, _s, _loop])
        _o = jnp.argsort(dst, stable=True)
        src = src[_o]
        dst = dst[_o]
        edge_attr_64 = 0.000189758 + 1.00013 * jax.random.normal(jax.random.fold_in(_gk, 12), (106250, 64), jnp.float32)
        return (x, src, dst, edge_attr_64)
    x, src, dst, edge_attr_64 = _rec_inputs()

    def _L0_gnn_setup():
        import jax, jax.numpy as jnp
        import numpy as np
        N_NODES = 3125
        N_EDGES = 37500
        D = 128
        EPS_MSG = 1e-07
        EPS_BN = 1e-05

        def _softmax_aggregate(msg, dst, n):
            m = jax.ops.segment_max(msg, dst, num_segments=n)
            ex = jnp.exp(msg - m[dst])
            denom = jax.ops.segment_sum(ex, dst, num_segments=n)
            alpha = ex / denom[dst]
            return jax.ops.segment_sum(msg * alpha, dst, num_segments=n)

        def _genconv(x, src, dst, W1, b1, g, be, W2, b2):
            n = x.shape[0]
            msg = jax.nn.relu(x[src]) + EPS_MSG
            out = _softmax_aggregate(msg, dst, n) + x
            h = out @ W1 + b1
            mu = h.mean(axis=0)
            var = h.var(axis=0)
            h = (h - mu) * jax.lax.rsqrt(var + EPS_BN) * g + be
            h = jax.nn.relu(h)
            return h @ W2 + b2
        key = jax.random.key(seed)
        ks = jax.random.split(key, 8)
        x = jax.random.normal(ks[0], (N_NODES, D), dtype=jnp.float32)
        src = jax.random.randint(ks[1], (N_EDGES,), 0, N_NODES)
        dst = jax.random.randint(ks[2], (N_EDGES,), 0, N_NODES)
        W1 = jax.random.normal(ks[3], (3, D, 2 * D), dtype=jnp.float32) * 0.05
        b1 = jnp.zeros((3, 2 * D), dtype=jnp.float32)
        gamma = jnp.ones((3, 2 * D), dtype=jnp.float32)
        beta = jnp.zeros((3, 2 * D), dtype=jnp.float32)
        W2 = jax.random.normal(ks[4], (3, 2 * D, D), dtype=jnp.float32) * 0.05
        b2 = jnp.zeros((3, D), dtype=jnp.float32)
        return {'x': x, 'W1': W1, 'b1': b1, 'gamma': gamma, 'beta': beta, 'W2': W2, 'b2': b2, 'src': src, 'dst': dst}
    _L0_gnn_all = _L0_gnn_setup()
    _L0_gnn_in = {k: v for k, v in _L0_gnn_all.items() if k in ('W1', 'b1', 'gamma', 'beta', 'W2', 'b2')}
    del _L0_gnn_all

    def _L1_gnn_setup():
        import jax, jax.numpy as jnp
        import numpy as np
        N = 3125
        E = 50000
        IN_N = 128
        IN_E = 64
        C = 128
        EPS = 1e-05

        def _lin_init(k, out_c, in_c):
            return jax.random.normal(k, (out_c, in_c), jnp.float32) / np.sqrt(in_c).astype(np.float32)

        def _layer(x, ea, src, dst, nw, ew, fnw, fnb, few, feb):
            h = jax.nn.relu(x @ nw.T)
            e = jax.nn.relu(ea @ ew.T)
            e2 = jnp.concatenate([h[src] + h[dst], e], axis=-1)
            agg = jax.ops.segment_sum(e, dst, num_segments=x.shape[0])
            n2 = jnp.concatenate([agg, h], axis=-1)
            n2 = jax.nn.relu(n2 @ fnw.T + fnb)
            e2 = jax.nn.relu(e2 @ few.T + feb)
            return (n2, e2)

        def _bn(x, g, b):
            return x * (g / jnp.sqrt(1.0 + EPS)) + b
        key = jax.random.key(seed)
        ks = iter(jax.random.split(key, 40))
        inp = {'x': jax.random.normal(next(ks), (N, IN_N), jnp.float32), 'edge_index': jax.random.randint(next(ks), (2, E), 0, N, jnp.int32), 'edge_attr': jax.random.normal(next(ks), (E, IN_E), jnp.float32)}
        in_dims = [(IN_N, IN_E), (C, C), (C, C)]
        for i, (inn, ine) in enumerate(in_dims):
            inp[f'nw{i}'] = _lin_init(next(ks), C // 2, inn)
            inp[f'ew{i}'] = _lin_init(next(ks), C // 2, ine)
            inp[f'fnw{i}'] = _lin_init(next(ks), C, C)
            inp[f'fnb{i}'] = jnp.zeros((C,), jnp.float32)
            inp[f'few{i}'] = _lin_init(next(ks), C, C)
            inp[f'feb{i}'] = jnp.zeros((C,), jnp.float32)
            inp[f'g{i}'] = jnp.ones((C,), jnp.float32)
            inp[f'b{i}'] = jnp.zeros((C,), jnp.float32)
        return inp
    _L1_gnn_all = _L1_gnn_setup()
    _L1_gnn_in = {k: v for k, v in _L1_gnn_all.items() if k in ('nw0', 'ew0', 'fnw0', 'fnb0', 'few0', 'feb0', 'g0', 'b0', 'nw1', 'ew1', 'fnw1', 'fnb1', 'few1', 'feb1', 'g1', 'b1', 'nw2', 'ew2', 'fnw2', 'fnb2', 'few2', 'feb2', 'g2', 'b2')}
    del _L1_gnn_all
    return {'x': x, 'src': src, 'dst': dst, 'edge_attr_64': edge_attr_64, 'L0_gnn_W1': _L0_gnn_in['W1'], 'L0_gnn_b1': _L0_gnn_in['b1'], 'L0_gnn_gamma': _L0_gnn_in['gamma'], 'L0_gnn_beta': _L0_gnn_in['beta'], 'L0_gnn_W2': _L0_gnn_in['W2'], 'L0_gnn_b2': _L0_gnn_in['b2'], 'L1_gnn_nw0': _L1_gnn_in['nw0'], 'L1_gnn_ew0': _L1_gnn_in['ew0'], 'L1_gnn_fnw0': _L1_gnn_in['fnw0'], 'L1_gnn_fnb0': _L1_gnn_in['fnb0'], 'L1_gnn_few0': _L1_gnn_in['few0'], 'L1_gnn_feb0': _L1_gnn_in['feb0'], 'L1_gnn_g0': _L1_gnn_in['g0'], 'L1_gnn_b0': _L1_gnn_in['b0'], 'L1_gnn_nw1': _L1_gnn_in['nw1'], 'L1_gnn_ew1': _L1_gnn_in['ew1'], 'L1_gnn_fnw1': _L1_gnn_in['fnw1'], 'L1_gnn_fnb1': _L1_gnn_in['fnb1'], 'L1_gnn_few1': _L1_gnn_in['few1'], 'L1_gnn_feb1': _L1_gnn_in['feb1'], 'L1_gnn_g1': _L1_gnn_in['g1'], 'L1_gnn_b1': _L1_gnn_in['b1'], 'L1_gnn_nw2': _L1_gnn_in['nw2'], 'L1_gnn_ew2': _L1_gnn_in['ew2'], 'L1_gnn_fnw2': _L1_gnn_in['fnw2'], 'L1_gnn_fnb2': _L1_gnn_in['fnb2'], 'L1_gnn_few2': _L1_gnn_in['few2'], 'L1_gnn_feb2': _L1_gnn_in['feb2'], 'L1_gnn_g2': _L1_gnn_in['g2'], 'L1_gnn_b2': _L1_gnn_in['b2']}

def reference(x, src, dst, edge_attr_64, L0_gnn_W1, L0_gnn_b1, L0_gnn_gamma, L0_gnn_beta, L0_gnn_W2, L0_gnn_b2, L1_gnn_nw0, L1_gnn_ew0, L1_gnn_fnw0, L1_gnn_fnb0, L1_gnn_few0, L1_gnn_feb0, L1_gnn_g0, L1_gnn_b0, L1_gnn_nw1, L1_gnn_ew1, L1_gnn_fnw1, L1_gnn_fnb1, L1_gnn_few1, L1_gnn_feb1, L1_gnn_g1, L1_gnn_b1, L1_gnn_nw2, L1_gnn_ew2, L1_gnn_fnw2, L1_gnn_fnb2, L1_gnn_few2, L1_gnn_feb2, L1_gnn_g2, L1_gnn_b2):
    import jax
    import jax.numpy as jnp

    def _L0_gnn_ref(x, W1, b1, gamma, beta, W2, b2, src, dst):
        import jax, jax.numpy as jnp
        import numpy as np
        N_NODES = 3125
        N_EDGES = 37500
        D = 128
        EPS_MSG = 1e-07
        EPS_BN = 1e-05

        def _softmax_aggregate(msg, dst, n):
            m = jax.ops.segment_max(msg, dst, num_segments=n)
            ex = jnp.exp(msg - m[dst])
            denom = jax.ops.segment_sum(ex, dst, num_segments=n)
            alpha = ex / denom[dst]
            return jax.ops.segment_sum(msg * alpha, dst, num_segments=n)

        def _genconv(x, src, dst, W1, b1, g, be, W2, b2):
            n = x.shape[0]
            msg = jax.nn.relu(x[src]) + EPS_MSG
            out = _softmax_aggregate(msg, dst, n) + x
            h = out @ W1 + b1
            mu = h.mean(axis=0)
            var = h.var(axis=0)
            h = (h - mu) * jax.lax.rsqrt(var + EPS_BN) * g + be
            h = jax.nn.relu(h)
            return h @ W2 + b2
        for i in range(3):
            x = _genconv(x, src, dst, W1[i], b1[i], gamma[i], beta[i], W2[i], b2[i])
            x = jax.nn.relu(x)
        return x

    def _L1_gnn_ref(x, edge_index, edge_attr, nw0, ew0, fnw0, fnb0, few0, feb0, g0, b0, nw1, ew1, fnw1, fnb1, few1, feb1, g1, b1, nw2, ew2, fnw2, fnb2, few2, feb2, g2, b2):
        import jax, jax.numpy as jnp
        import numpy as np
        N = 3125
        E = 50000
        IN_N = 128
        IN_E = 64
        C = 128
        EPS = 1e-05

        def _lin_init(k, out_c, in_c):
            return jax.random.normal(k, (out_c, in_c), jnp.float32) / np.sqrt(in_c).astype(np.float32)

        def _layer(x, ea, src, dst, nw, ew, fnw, fnb, few, feb):
            h = jax.nn.relu(x @ nw.T)
            e = jax.nn.relu(ea @ ew.T)
            e2 = jnp.concatenate([h[src] + h[dst], e], axis=-1)
            agg = jax.ops.segment_sum(e, dst, num_segments=x.shape[0])
            n2 = jnp.concatenate([agg, h], axis=-1)
            n2 = jax.nn.relu(n2 @ fnw.T + fnb)
            e2 = jax.nn.relu(e2 @ few.T + feb)
            return (n2, e2)

        def _bn(x, g, b):
            return x * (g / jnp.sqrt(1.0 + EPS)) + b
        src, dst = (edge_index[0], edge_index[1])
        layers = [(nw0, ew0, fnw0, fnb0, few0, feb0, g0, b0), (nw1, ew1, fnw1, fnb1, few1, feb1, g1, b1), (nw2, ew2, fnw2, fnb2, few2, feb2, g2, b2)]
        ea = edge_attr
        for nw, ew, fnw, fnb, few, feb, g, b in layers:
            x, ea = _layer(x, ea, src, dst, nw, ew, fnw, fnb, few, feb)
            x = _bn(x, g, b)
        return x
    edge_index = jnp.stack([src, dst])
    h = jnp.maximum(_layernorm(x, axis=-1), 0.0)
    x = x + _L0_gnn_ref(h, L0_gnn_W1, L0_gnn_b1, L0_gnn_gamma, L0_gnn_beta, L0_gnn_W2, L0_gnn_b2, src, dst)
    h = jnp.maximum(_layernorm(x, axis=-1), 0.0)
    x = x + _L1_gnn_ref(h, edge_index, edge_attr_64, L1_gnn_nw0, L1_gnn_ew0, L1_gnn_fnw0, L1_gnn_fnb0, L1_gnn_few0, L1_gnn_feb0, L1_gnn_g0, L1_gnn_b0, L1_gnn_nw1, L1_gnn_ew1, L1_gnn_fnw1, L1_gnn_fnb1, L1_gnn_few1, L1_gnn_feb1, L1_gnn_g1, L1_gnn_b1, L1_gnn_nw2, L1_gnn_ew2, L1_gnn_fnw2, L1_gnn_fnb2, L1_gnn_few2, L1_gnn_feb2, L1_gnn_g2, L1_gnn_b2)
    return x

_drawn_inputs = setup_inputs


def setup_inputs(seed=0):
    import zlib

    import numpy as np

    out = dict(_drawn_inputs(seed))
    spreads = {'L0_gnn_b1': (0.0, 2.0),
     'L0_gnn_gamma': (1.0, 0.6),
     'L0_gnn_beta': (0.0, 0.8),
     'L0_gnn_b2': (0.0, 0.8),
     'L1_gnn_fnb0': (0.0, 0.428),
     'L1_gnn_feb0': (0.0, 0.8),
     'L1_gnn_g0': (1.0, 0.2),
     'L1_gnn_b0': (0.0, 0.364),
     'L1_gnn_fnb1': (0.0, 2.0),
     'L1_gnn_feb1': (0.0, 0.326),
     'L1_gnn_g1': (1.0, 0.6),
     'L1_gnn_b1': (0.0, 2.0),
     'L1_gnn_fnb2': (0.0, 0.8),
     'L1_gnn_feb2': (0.0, 0.1),
     'L1_gnn_g2': (1.0, 0.2),
     'L1_gnn_b2': (0.0, 0.8)}
    factors = {}
    for name, (base, spread) in spreads.items():
        noise = np.random.default_rng([zlib.crc32(name.encode()), seed]).standard_normal(out[name].shape)
        drawn = base * np.exp(spread * noise) if base else spread * noise
        out[name] = jnp.asarray(drawn.astype(out[name].dtype))
    for name, factor in factors.items():
        out[name] = (out[name] * factor).astype(out[name].dtype)
    return out
```

```python
from contextlib import ExitStack

import concourse.bass as bass
from concourse import mybir

F32, I32, BF16 = mybir.dt.float32, mybir.dt.int32, mybir.dt.bfloat16
ALU = mybir.AluOpType
ACT = mybir.ActivationFunctionType
AX = mybir.AxisListType.X

N, E, D, DE, HID, HALF = 6250, 106250, 128, 64, 256, 64
L = 3
P = 128
TILE = 125
CH = 250
NCH = N // CH
J = 4
GE = P * J
NG = -(-E // GE)
LAST = E - (NG - 1) * GE
W = P // 3
NP = N + W
GT = NG // 2
RING = 8
EPS_MSG, EPS = 1e-7, 1e-5
TINY = 1e-37
RANGE = 60.0


class At:

    def __init__(self, base, off):
        self.base, self.off = base, off

    def __sub__(self, lag):
        return At(self.base, self.off - lag)

    def inside(self, n):
        return self.base is not None or 0 <= self.off < n

    def times(self, m, c=0):
        return self.off * m + c if self.base is None else self.base * m + (self.off * m + c)


def pipeline(e, n, unroll, peel, tail, body):
    end = peel + (n - peel - 1) // unroll * unroll
    for i in range(peel):
        body(At(None, i))
    with e.Fori(peel, end, unroll) as base:
        base = e.bass.s_assert_within(base, peel, end - unroll,
                                      skip_runtime_bounds_check_because="the loop counts by its step")
        for u in range(unroll):
            body(At(base, u))
    for i in range(end, n + tail):
        body(At(None, i))


def wait(e, sem, i, m=1, c=None):
    v = i.times(m, m if c is None else c)
    if not isinstance(v, int) or v > 0:
        e.wait_ge(sem, v)


def gnn_kernel(nc, a, out):
    with ExitStack() as ctx:
        def sb(name, shape, dt=F32):
            return ctx.enter_context(nc.sbuf_tensor(name, shape, dt))

        def sem(name):
            return ctx.enter_context(nc.semaphore(name))

        def dram(name, shape, dt=F32):
            return nc.dram_tensor(name, shape, dt, kind="Internal").ap()

        x_mid = dram("x_mid", [N, D])
        msg_table = dram("msg_table", [N, D])
        h_table = dram("h_table", [N, D])
        h_parts = dram("h_parts", [3, NP, D], BF16)
        e0_rows = dram("e0_rows", [NG, P, J * HALF])
        dst_pad = dram("dst_pad", [NG, GE], I32)
        rel_rows = dram("rel_rows", [NG, J, P], BF16)

        xT_all = sb("xT", [P, 2 * NCH * D])
        xT = xT_all[:, 0:N]
        acc = sb("acc", [P, 2, NP])
        hid = acc
        x_rows = acc[0:TILE, :, :].rearrange("p k n -> p (k n)")[:, 0:2 * NCH * D].rearrange("p (t d) -> p t d", d=D)
        nw1_pair = sb("nw1_pair", [P, P])
        ew1_pair = sb("ew1_pair", [P, P])
        ew2_pair = sb("ew2_pair", [P, P])
        ew0_pair = sb("ew0_pair", [P, P])
        Z0 = sb("Z0", [P, NP])
        Z1, Z2 = acc[:, 0, :], acc[:, 1, :]
        ring = sb("ring", [P, RING, J, 320])
        msg = ring[:, :, :, 0:D]
        ex = ring[:, :, :, D:2 * D]
        onehot = sb("onehot", [P, RING, J, P])
        onehotT = sb("onehotT", [3 * W, 4, GE], BF16)
        window = sb("window", [3 * W, RING, D], BF16)
        relb = sb("relb", [3 * W, 4, GE], BF16)
        work = sb("work", [P, 6, GE])
        src_idx = sb("src_idx", [P, NG, J], I32)
        idx_ring = sb("idx_ring", [P, RING, J], I32)
        rel = sb("rel", [P, NG, J])
        starts = sb("starts", [1, NG], I32)
        shifts = sb("shifts", [1, NG], I32)
        slot = ring[:, :, :, :].rearrange("p s j c -> p s (j c)")
        idx_i, idx2 = (slot[0:GT, s, 0:2 * GE].bitcast(I32).rearrange("g (k q) -> g k q", k=2) for s in (0, 1))
        relw = slot[0:GT, 2, 0:GE].bitcast(BF16).rearrange("g (k q) -> g k q", k=2)
        idx_f = work[0:GT, 0:4, :]
        ident = sb("ident", [P, P])
        iota_w = sb("iota_w", [P, W])
        iota_p = sb("iota_p", [P, 1])
        iota_t = sb("iota_t", [P, 4])
        ones = sb("ones", [1, P])
        stat = sb("stat", [P, 2, NCH, 6])
        mv = sb("mv", [P, 3, 2 * NCH])
        rstat = work[0:TILE, 4, 0:2 * NCH * 6].rearrange("p (t s) -> p t s", s=6)
        add_rows = xT_all[0:TILE, :].rearrange("p (t d) -> p t d", d=D)
        sc = sb("sc", [P, 2 * NCH])
        sh = sb("sh", [P, 2 * NCH])
        cmax = sb("cmax", [P, NCH])
        small = sb("small", [P, 16])
        row = sb("row", [1, 2, NG])
        negc = sb("negc", [P, 1])
        flag = sb("flag", [1, 2], I32)
        W1 = sb("W1", [P, HID])
        W2 = sb("W2", [P, 2, D])
        b1, gam, bet = (sb(n, [P, 2]) for n in ("b1", "gam", "bet"))
        b2 = sb("b2", [P, 1])
        vecs = sb("vecs", [P, 4 * L])
        wraw = slot[:, 3:6, :].rearrange("p s q -> p (s q)")[:, 0:11 * P].rearrange("p (n c) -> p n c", n=11)
        lin = {n: sb(n, [P, P]) for n in ("nw0", "few0", "few1", "fnw0", "fnw1", "fnw2")}
        lin |= {n: sb(n, [P, HALF]) for n in ("nw1", "nw2", "ew0", "ew1", "ew2")}

        ps = [ctx.enter_context(nc.psum_tensor(f"ps{i}", [P, 512], F32)) for i in range(8)]


        def cols(i):
            return bass.ds(i.times(CH), CH) if not isinstance(i.times(CH), int) else slice(i.off * CH, (i.off + 1) * CH)

        def rows_of(t, i):
            v = t.rearrange("(c k p) d -> c p k d", p=TILE, k=2)
            return v[i.off, :, :, :] if i.base is None else v[bass.ds(i.times(1), 1), :, :, :].rearrange("o p k d -> (o p) k d")

        def pair(k, width=CH):
            return [work[:, k, b * 256:b * 256 + width] for b in range(2)]

        def rowring(k):
            return [work[0:TILE, k + b // 2, b % 2 * 256:b % 2 * 256 + 2 * D].rearrange("p (k d) -> p k d", k=2) for b in range(4)]

        def stores(e, S, names, n):
            for b, name in enumerate(names):
                e.wait_ge(S(name), 16 * len(range(b, n, len(names))))

        def begin(e, S):
            e.sem_inc(S("issued"), 1)

        phases = []
        TABLE = ["table0", "table1", "table2", "table3"]

        MATS = [("nw0", 0), ("nw1", 0), ("nw2", 0), ("ew0", 0), ("ew1", 0), ("ew2", 0),
                ("few0", 1), ("few1", 0), ("fnw0", 0), ("fnw1", 0), ("fnw2", 1)]

        def setup_sync(e, S):
            e.wait_ge(S("pads"), 2)
            for k, name in enumerate(("src", "dst")):
                for h, t in enumerate((idx_i, idx2)):
                    full = GT if h == 0 else NG - 1 - GT
                    v = a[name][h * GT * GE:(h * GT + full) * GE].rearrange("(g q) -> g q", q=GE)
                    e.dma_start(t[0:full, k, :], v).then_inc(S("indices"), 16)
                e.dma_start(idx2[GT - 1:GT, k, 0:LAST],
                            a[name][(NG - 1) * GE:E].rearrange("(g q) -> g q", g=1)).then_inc(S("indices"), 16)
            e.dma_start(starts[:, :], a["dst"][0:(NG - 1) * GE + 1:GE].rearrange("(g q) -> g q", g=1),
                        allow_slow_non_contiguous=True).then_inc(S("starts"), 16)
            e.wait_ge(S("indices"), 16 * 6)
            for h, t in enumerate((idx_i, idx2)):
                e.dma_start(dst_pad[h * GT:(h + 1) * GT, :], t[:, 1, :]).then_inc(S("pad_out"), 16)
            for l in range(L):
                for k, n in enumerate(("fnb", "feb", "g", "b")):
                    e.dma_start(vecs[:, 4 * l + k:4 * l + k + 1],
                                a[f"L1_gnn_{n}{l}"].rearrange("(k o) -> k o", o=1)).then_inc(S("vecs"), 16)
            for n, (name, swap) in enumerate(MATS):
                w = a["L1_gnn_" + name]
                r, c = w.shape
                halves = ((HALF, 0) if swap else (0, HALF)) if c > HALF else (0, 0)
                for k, c0 in enumerate(halves):
                    e.dma_start(wraw[0:r, n, k * HALF:(k + 1) * HALF], w[:, c0:c0 + HALF]).then_inc(S("weights"), 16)
            for h in range(2):
                e.wait_ge(S("relw"), h + 1)
                e.dma_start(rel_rows[h * GT:(h + 1) * GT, :, :].rearrange("g j p -> g (j p)"),
                            relw[:, h, :]).then_inc(S("rel_out"), 16)
            e.wait_ge(S("rel_out"), 32)
            e.wait_ge(S("pad_out"), 32)
            e.wait_ge(S("vecs"), 16 * 4 * L)
            e.wait_ge(S("starts"), 16)

        def setup_pool(e, S):
            e.memset(ident[:, :], 1.0).then_inc(S("const"), 1)
            e.wait_ge(S("const"), 1)
            e.affine_select(out=ident[:, :], in_=ident[:, :], compare_op=ALU.is_equal, fill=0.0, base=0,
                            pattern=[[-1, P]], channel_multiplier=1).then_inc(S("const"), 1)
            e.iota(iota_w[:, :], pattern=[[1, W]], base=0, channel_multiplier=0,
                   allow_small_or_imprecise_dtypes=True).then_inc(S("const"), 1)
            e.iota(iota_t[:, 0:1], pattern=[[0, 1]], base=0, channel_multiplier=1,
                   allow_small_or_imprecise_dtypes=True).then_inc(S("const"), 1)
            e.memset(ones[:, :], 1.0).then_inc(S("const"), 1)
            e.memset(Z0[:, :], 0.0).then_inc(S("const"), 1)
            e.memset(ew0_pair[:, :], 0.0).then_inc(S("const"), 1)
            e.memset(xT_all[:, N:NP], 0.0).then_inc(S("zeros"), 1)
            e.memset(onehot[:, :, :, :], 0.0).then_inc(S("zeros"), 1)
            e.wait_ge(S("zeros"), 2)

        def setup_pe(e, S):
            e.wait_ge(S("const"), 7)
            e.wait_ge(S("weights"), 32 * len(MATS))
            for n, (name, _) in enumerate(MATS):
                r = a["L1_gnn_" + name].shape[0]
                if n >= 2:
                    e.wait_ge(S("turned_copy"), n - 1)
                e.transpose(ps[n % 2][:, 0:r], wraw[0:r, n, :], ident[0:r, 0:r]).then_inc(S("turned"), 1)
            e.wait_ge(S("idx_f"), 2)
            for n in range(4 * J):
                h, k, j = n // (2 * J), n // J % 2, n % J
                if n >= 2:
                    e.wait_ge(S("idx_copy"), n - 1)
                e.transpose(ps[2 + n % 2][:, 0:GT], idx_f[:, 2 * h + k, j:GE:J],
                            ident[0:GT, 0:GT]).then_inc(S("idx_turned"), 1)
            e.wait_ge(S("worst"), 1)
            e.transpose(ps[4][0:1, 0:GT], small[0:GT, 8:9], ident[0:GT, 0:GT]).then_inc(S("worst_row"), 1)

        def setup_dve(e, S):
            def then(ins):
                ins.then_inc(S("v"), 1)
                then.n += 1
                e.wait_ge(S("v"), then.n)
            then.n = 0
            e.memset(idx2[:, 0, :], 0).then_inc(S("pads"), 1)
            e.memset(idx2[:, 1, :], N).then_inc(S("pads"), 1)
            e.wait_ge(S("const"), 7)
            then(e.tensor_scalar(iota_t[:, 1:2], iota_t[:, 0:1], float(W), -float(W), ALU.is_ge, ALU.mult))
            then(e.tensor_scalar(iota_t[:, 2:3], iota_t[:, 0:1], 2.0 * W, -float(W), ALU.is_ge, ALU.mult))
            then(e.tensor_tensor(iota_t[:, 3:4], iota_t[:, 1:2], iota_t[:, 2:3], ALU.add))
            then(e.tensor_tensor(iota_p[:, :], iota_t[:, 0:1], iota_t[:, 3:4], ALU.add))
            e.wait_ge(S("indices"), 16 * 6)
            then(e.tensor_copy(idx_f[:, 0:2, :], idx_i))
            then(e.tensor_copy(idx_f[:, 2:4, :], idx2))
            for h in range(2):
                then(e.tensor_copy(small[0:GT, h:h + 1], idx_f[:, 2 * h + 1, 0:1]))
                e.tensor_scalar(idx_f[:, 2 * h + 1, :], idx_f[:, 2 * h + 1, :], small[0:GT, h:h + 1], None,
                                ALU.subtract).then_inc(S("idx_f"), 1)
                e.wait_ge(S("idx_f"), h + 1)
                e.tensor_copy(relw[:, h, :].rearrange("g (j p) -> g j p", j=J),
                              idx_f[:, 2 * h + 1, :].rearrange("g (p j) -> g j p", j=J)).then_inc(S("relw"), 1)
            for h in range(2):
                then(e.tensor_reduce(small[0:GT, 2 + h:3 + h], idx_f[:, 2 * h + 1, :], AX, ALU.max))
                then(e.tensor_reduce(small[0:GT, 4 + h:5 + h], idx_f[:, 2 * h + 1, :], AX, ALU.min))
                then(e.tensor_scalar(small[0:GT, 4 + h:5 + h], small[0:GT, 4 + h:5 + h], -float(W), None, ALU.mult))
            then(e.tensor_reduce(small[0:GT, 8:9], small[0:GT, 2:6], AX, ALU.max))
            e.sem_inc(S("worst"), 1)
            for n, (name, _) in enumerate(MATS):
                r = a["L1_gnn_" + name].shape[0]
                e.wait_ge(S("turned"), n + 1)
                e.tensor_copy(lin[name][:, 0:r], ps[n % 2][:, 0:r]).then_inc(S("turned_copy"), 1)
            then(e.tensor_copy(lin["nw0"][:, HALF:P], lin["nw0"][:, 0:HALF]))
            for name, pair in (("nw1", nw1_pair), ("ew1", ew1_pair), ("ew2", ew2_pair)):
                for h in (slice(0, HALF), slice(HALF, P)):
                    then(e.tensor_copy(pair[:, h], lin[name][:, :]))
            for h in (slice(0, HALF), slice(HALF, P)):
                then(e.tensor_copy(ew0_pair[h, h], lin["ew0"][h, :]))
            for n in range(4 * J):
                h, k, j = n // (2 * J), n // J % 2, n % J
                e.wait_ge(S("idx_turned"), n + 1)
                e.tensor_copy((rel if k else src_idx)[:, h * GT:(h + 1) * GT, j],
                              ps[2 + n % 2][:, 0:GT]).then_inc(S("idx_copy"), 1)
            e.wait_ge(S("worst_row"), 1)
            then(e.tensor_reduce(small[0:1, 9:10], ps[4][0:1, 0:GT], AX, ALU.max))
            then(e.tensor_scalar(small[0:1, 10:11], small[0:1, 9:10], float(W), None, ALU.is_ge))
            then(e.tensor_copy(flag[0:1, 1:2], small[0:1, 10:11]))
            e.wait_ge(S("starts"), 16)
            then(e.tensor_copy(row[:, 0, :], starts[:, :]))
            then(e.memset(row[:, 1, :], 0.0))
            then(e.tensor_tensor(row[:, 1, 1:NG], row[:, 0, 1:NG], row[:, 0, 0:NG - 1], ALU.subtract))
            then(e.tensor_scalar(row[:, 1, :], row[:, 1, :], float(W), 0.0, ALU.min, ALU.max))
            then(e.tensor_copy(shifts[:, :], row[:, 1, :]))
            e.wait_ge(S("vecs"), 16 * 4 * L)
            for l in range(L):
                g = vecs[:, 4 * l + 2:4 * l + 3]
                then(e.tensor_scalar(g, g, (1.0 + EPS) ** -0.5, None, ALU.mult))

        SETUP = "pad_out zeros pads indices starts vecs weights relw rel_out const turned turned_copy idx_f idx_copy idx_turned worst worst_row v".split()
        phases.append(("setup", SETUP, dict(sync=setup_sync, pool=setup_pool, pe=setup_pe, dve=setup_dve)))

        def shift_pe(e, S):
            e.wait_ge(S("max_col"), 1)
            e.transpose(ps[2][0:1, 0:P], small[:, 11:12], ident[:, :]).then_inc(S("max_row"), 1)
            e.wait_ge(S("max_one"), 1)
            e.matmul(ps[3][:, 0:1], ones[:, :], small[0:1, 12:13], start=True, stop=True).then_inc(S("max_all"), 1)

        def shift_dve(e, S):
            e.tensor_reduce(small[:, 11:12], cmax[:, :], AX, ALU.max).then_inc(S("max_col"), 1)
            e.wait_ge(S("max_row"), 1)
            e.tensor_reduce(small[0:1, 12:13], ps[2][0:1, 0:P], AX, ALU.max).then_inc(S("max_one"), 1)
            e.wait_ge(S("max_all"), 1)
            e.tensor_scalar(negc[:, :], ps[3][:, 0:1], -1.0, None, ALU.mult).then_inc(S("shift"), 1)
            e.tensor_scalar(small[0:1, 13:14], small[0:1, 12:13], RANGE, small[0:1, 10:11], ALU.is_gt, ALU.max).then_inc(S("shift"), 1)
            e.wait_ge(S("shift"), 2)
            e.tensor_copy(flag[0:1, 0:1], small[0:1, 13:14]).then_inc(S("shift"), 1)

        SHIFT = "max_col max_row max_one max_all shift".split()

        def norm_phase(first):
            hrow = rowring(0)

            def sync(e, S):
                e.dma_start(x_rows, a["x"].rearrange("(t p) d -> p t d", p=TILE)).then_inc(S("rows"), 16)
                if not first:
                    e.dma_start(add_rows, msg_table.rearrange("(t p) d -> p t d", p=TILE)).then_inc(S("rows"), 16)
                    e.wait_ge(S("sum"), 1)
                    e.dma_start(x_mid.rearrange("(t p) d -> p t d", p=TILE), x_rows).then_inc(S("mid"), 16)
                    e.wait_ge(S("mid"), 16)
                else:
                    def step(i):
                        wait(e, S("h"), i)
                        begin(e, S)
                        e.dma_start(rows_of(msg_table, i), hrow[i.off % 4]).then_inc(S(TABLE[i.off % 4]), 16)
                    pipeline(e, NCH, 4, 4, 0, step)
                    stores(e, S, TABLE, NCH)

            def dve(e, S):
                e.wait_ge(S("rows"), 16 if first else 32)
                if not first:
                    e.tensor_tensor(x_rows, x_rows, add_rows, ALU.add).then_inc(S("sum"), 1)
                    e.wait_ge(S("sum"), 1)

                def stats(i):
                    if i.base is None:
                        e.bn_stats(rstat[:, i.off, :], x_rows[:, i.off, :]).then_inc(S("stats"), 1)
                    else:
                        e.bn_stats(rstat[:, bass.ds(i.times(1), 1), :].rearrange("p o s -> p (o s)"),
                                   x_rows[:, bass.ds(i.times(1), 1), :].rearrange("p o d -> p (o d)")).then_inc(S("stats"), 1)

                pipeline(e, 2 * NCH, 2, 2, 0, stats)
                e.wait_ge(S("stats"), 2 * NCH)
                v = [0]

                def then(ins):
                    v[0] += 1
                    ins.then_inc(S("scale"), 1)
                    e.wait_ge(S("scale"), v[0])
                m0, q0, m1, q1 = (rstat[:, :, k] for k in (1, 2, 4, 5))
                mean, var, diff = (mv[0:TILE, k, :] for k in range(3))
                then(e.tensor_tensor(mean, m0, m1, ALU.add))
                then(e.tensor_scalar(mean, mean, 0.5, None, ALU.mult))
                then(e.tensor_tensor(diff, m0, m1, ALU.subtract))
                then(e.tensor_scalar(diff, diff, 0.5, None, ALU.mult))
                then(e.tensor_tensor(diff, diff, diff, ALU.mult))
                then(e.tensor_tensor(var, q0, q1, ALU.add))
                then(e.tensor_scalar(var, var, 1.0 / D, EPS, ALU.mult, ALU.add))
                then(e.tensor_tensor(sc[0:TILE, :], var, diff, ALU.add))
                e.sem_inc(S("var"), 1)
                e.wait_ge(S("root"), 1)
                then(e.reciprocal(sc[0:TILE, :], sc[0:TILE, :]))
                then(e.tensor_tensor(sh[0:TILE, :], mean, sc[0:TILE, :], ALU.mult))
                then(e.tensor_scalar(sh[0:TILE, :], sh[0:TILE, :], -1.0, None, ALU.mult))
                e.sem_inc(S("norm"), 1)

                def copy(i):
                    if i.inside(NCH):
                        wait(e, S("turn"), i)
                        e.tensor_copy(xT[:, cols(i)], ps[i.off % 2][:, 0:CH]).then_inc(S("xT"), 1)
                    if (i - 1).inside(NCH):
                        wait(e, S("xT"), i - 1)
                        k = i - 1
                        c = slice(k.off, k.off + 1) if k.base is None else bass.ds(k.times(1), 1)
                        e.tensor_reduce(cmax[:, c], xT[:, cols(k)], AX, ALU.max).then_inc(S("cmax"), 1)
                pipeline(e, NCH, 2, 2, 1, copy)
                e.wait_ge(S("cmax"), NCH)
                if first:
                    shift_dve(e, S)

            def act(e, S):
                e.wait_ge(S("var"), 1)
                e.activation(sc[0:TILE, :], sc[0:TILE, :], ACT.Sqrt).then_inc(S("root"), 1)
                e.wait_ge(S("norm"), 1)

                def step(i):
                    wait(e, S("turn"), i - 4)
                    if first:
                        wait(e, S(TABLE[i.off % 4]), i, 4, -4 * (i.off % 4))
                    for k in range(2):
                        t = 2 * i.off + k
                        if i.base is None:
                            src, s1, s2 = x_rows[:, t, :], sc[0:TILE, t:t + 1], sh[0:TILE, t:t + 1]
                        else:
                            q = bass.ds(i.times(2, k), 1)
                            src = x_rows[:, q, :].rearrange("p o d -> p (o d)")
                            s1, s2 = sc[0:TILE, q], sh[0:TILE, q]
                        ins = e.activation(hrow[i.off % 4][:, k, :], src, ACT.Relu, bias=s2, scale=s1)
                    ins.then_inc(S("h"), 1)
                pipeline(e, NCH, 4, 4, 0, step)

            def pe(e, S):
                def step(i):
                    wait(e, S("h"), i)
                    wait(e, S("xT"), i - 2)
                    for k in range(2):
                        ins = e.transpose(ps[i.off % 2][:, k * TILE:(k + 1) * TILE], hrow[i.off % 4][:, k, :],
                                          ident[0:TILE, 0:TILE])
                    ins.then_inc(S("turn"), 1)
                pipeline(e, NCH, 4, 4, 0, step)
                if first:
                    shift_pe(e, S)

            names = "issued rows sum mid table0 table1 table2 table3 stats var root scale norm h turn xT cmax".split() + SHIFT
            return ("norm", names, dict(sync=sync, act=act, pe=pe, dve=dve))

        phases.append(norm_phase(True))

        def hidden_general(who, e, S):
            quot = [work[:, b, 0:CH] for b in range(2)]
            if who == "dve":
                def step(i):
                    b = quot[i.off % 2]
                    wait(e, S("W1"), i - 2)
                    e.reciprocal(b, acc[:, 0, cols(i)]).then_inc(S("quot"), 1)
                    wait(e, S("quot"), i, 3, 1)
                    e.tensor_tensor(b, b, acc[:, 1, cols(i)], ALU.mult).then_inc(S("quot"), 1)
                    wait(e, S("quot"), i, 3, 2)
                    e.tensor_tensor(b, b, xT[:, cols(i)], ALU.add).then_inc(S("quot"), 1)
                pipeline(e, NCH, 2, 2, 0, step)
            if who == "pe":
                def step(i):
                    wait(e, S("quot"), i, 3)
                    wait(e, S("hid"), i - 2)
                    for h in range(2):
                        ins = e.matmul(ps[i.off % 2][:, h * 256:h * 256 + CH], W1[:, h * P:(h + 1) * P], quot[i.off % 2],
                                       start=True, stop=True)
                    ins.then_inc(S("W1"), 1)
                pipeline(e, NCH, 2, 2, 0, step)
            if who == "act":
                hidden_columns(e, S)

        def hidden_columns(e, S):
            def step(i):
                wait(e, S("W1"), i)
                for h in range(2):
                    ins = e.activation(hid[:, h, cols(i)], ps[i.off % 2][:, h * 256:h * 256 + CH], ACT.Identity,
                                       bias=b1[:, h:h + 1])
                ins.then_inc(S("hid"), 1)
            pipeline(e, NCH, 2, 2, 0, step)

        drow = sb("drow", [1, GE], I32)
        dst_cols = sb("dst_cols", [P, 2 * J], I32)
        greatest = slot[:, 2:8, :].rearrange("p s q -> p (s q)")[:, 0:NP]

        def relay(sweeps):
            def part(who, e, S):
                before = 1
                if who == "dve":
                    e.sem_inc(S("baton"), 1)
                for turns in sweeps:
                    def lap(g):
                        for k, (owner, step) in enumerate(turns):
                            if owner == who:
                                e.wait_ge(S("baton"), g.times(len(turns), k + before))
                                begin(e, S)
                                step(e, S, g)
                                begin(e, S)
                                e.drain()
                                e.sem_inc(S("baton"), 1)
                    with e.Fori(0, NG - 1, 1) as base:
                        lap(At(base, 0))
                    lap(At(None, NG - 1))
                    before += len(turns) * NG
                e.wait_ge(S("baton"), before)
                e.drain()
            return part

        def either(column, general, parts):
            def of(who):
                def run(e, S):
                    needed = e.value_load(flag[0:1, column:column + 1], min_val=0, max_val=1)
                    with e.If(needed):
                        general(who, e, S)
                    with e.Else():
                        parts[who](e, S)
                return run
            return {who: of(who) for who in ("sync", "pool", "act", "pe", "dve")}

        def bias(l, k):
            return vecs[:, 4 * l + k:4 * l + k + 1]

        def one(g):
            return bass.ds(g.times(1), 1)

        def serial(e, per_edge):
            with e.Fori(0, P, 1) as p:
                for j in range(J):
                    d = e.value_load(drow[0:1, bass.ds(p * J + j, 1)], min_val=0, max_val=N)
                    per_edge(bass.ds(p + j * P, 1), bass.ds(d, 1))
                    e.drain()

        def all_gather(name, jobs):
            def step(e, S, g):
                for table, dst, idx in jobs:
                    for j in range(J):
                        e.indirect_dma_start(out=dst[:, j, :], out_offset=None, in_=table,
                                             in_offset=bass.IndirectOffsetOnAxis(ap=idx[:, j:j + 1], axis=0)
                                             ).then_inc(S("gather_all_" + name), 16)
                m = 16 * J * len(jobs)
                e.wait_ge(S("gather_all_" + name), g.times(m, m))
            return step

        def take_sources(e, S, g):
            e.activation(idx_ring[:, 0, :].rearrange("p (o j) -> p o j", o=1), src_idx[:, one(g), :], ACT.Copy)

        def take_destinations(name):
            def step(e, S, g):
                e.dma_start(drow[:, :], dst_pad[one(g), :]).then_inc(S(name), 16)
                e.wait_ge(S(name), g.times(16, 16))
            return step

        def turn_rows(bank, rows, width=P):
            def step(e, S, g):
                for j in range(J):
                    e.transpose(bank[0:width, j * P:(j + 1) * P], rows[:, j, :], ident[:, :])
            return step

        def edges_general(layer, attr):
            m, ex_m, exps = work[:, 0, :], work[:, 1:3, :], work[:, 1, :]
            ea, eaT = (work[:, k, 0:2 * P] for k in (3, 4))
            e0T = work[0:HALF, 5, :]
            er = ring[:, 1, :, 2 * D:2 * D + HALF]

            def maxima(e, S, g):
                e.tensor_scalar(m, ps[0][:, :], EPS_MSG, None, ALU.add)
                e.drain()
                serial(e, lambda c, d: e.tensor_tensor(greatest[:, d], greatest[:, d], m[:, c], ALU.max))

            def minus(e, S, g):
                e.tensor_scalar(m, ps[0][:, :], EPS_MSG, None, ALU.add)
                e.drain()
                serial(e, lambda c, d: e.tensor_tensor(exps[:, c], m[:, c], greatest[:, d], ALU.subtract))

            def exp(e, S, g):
                e.activation(exps, exps, ACT.Exp)

            def sums(e, S, g):
                e.tensor_tensor(work[:, 2, :], exps, m, ALU.mult)
                e.drain()
                serial(e, lambda c, d: e.tensor_tensor(acc[:, :, d], acc[:, :, d], ex_m[:, :, c], ALU.add))

            def load_attr(e, S, g):
                v = ea.rearrange("p (j c) -> p j c", j=J)
                if g.base is None:
                    full = LAST // J
                    src = a["edge_attr_64"][(NG - 1) * GE:(NG - 1) * GE + full * J, :]
                    e.dma_start(v[0:full, :, :], src.rearrange("(p j) c -> p j c", j=J)).then_inc(S("all_ea"), 16)
                    e.dma_start(v[full:full + 1, 0:LAST - full * J, :],
                                a["edge_attr_64"][E - (LAST - full * J):E, :].rearrange("(o j) c -> o j c", o=1)).then_inc(S("all_ea"), 16)
                else:
                    e.dma_start(v, a["edge_attr_64"][bass.ds(g.times(GE), GE), :].rearrange("(p j) c -> p j c", j=J)).then_inc(S("all_ea"), 16)
                e.wait_ge(S("all_ea"), g.times(16, 16) if g.base is not None else 16 * (NG + 1))

            def turn_attr(e, S, g):
                for h in range(J // 2):
                    e.transpose(ps[2][:, h * P:(h + 1) * P], ea[:, h * P:(h + 1) * P], ident[:, :])

            def copy_attr(e, S, g):
                e.activation(eaT, ps[2][:, 0:2 * P], ACT.Copy)

            def first_layer(e, S, g):
                for h in range(J // 2):
                    e.matmul(ps[4][:, h * P:(h + 1) * P], eaT[:, h * P:(h + 1) * P], ew0_pair[:, :], start=True, stop=True)

            def relu_e0(e, S, g):
                e.tensor_scalar(er, ps[4][:, 0:J * HALF].rearrange("p (j c) -> p j c", j=J), 0.0, None, ALU.max)

            def store_e0(e, S, g):
                e.dma_start(e0_rows[one(g), :, :].rearrange("o p c -> (o p) c").rearrange("p (j c) -> p j c", j=J),
                            er).then_inc(S("all_e0"), 16)
                e.wait_ge(S("all_e0"), g.times(16, 16))

            def sum_e0(e, S, g):
                e.tensor_copy(e0T, ps[5][0:HALF, :])
                e.drain()
                serial(e, lambda c, d: e.tensor_tensor(Z0[0:HALF, d], Z0[0:HALF, d], e0T[:, c], ALU.add))

            def fetch(k):
                return [("act", take_sources), ("sync", take_destinations(f"all_dst{k}")),
                        ("pool", all_gather(f"{layer}_{k}", [(msg_table, msg[:, 0, :, :], idx_ring[:, 0, :])])),
                        ("pe", turn_rows(ps[0], msg[:, 0, :, :]))]
            sweeps = [fetch(0) + [("dve", maxima)],
                      fetch(1) + [("dve", minus), ("act", exp), ("dve", sums)]]
            if attr:
                sweeps.append([("sync", load_attr), ("pe", turn_attr), ("act", copy_attr), ("pe", first_layer), ("dve", relu_e0),
                               ("sync", store_e0), ("sync", take_destinations("all_dst2")), ("pe", turn_rows(ps[5], er, HALF)),
                               ("dve", sum_e0)])
            passes = relay(sweeps)

            def part(who, e, S):
                if who == "dve":
                    e.memset(greatest, 0.0)
                    e.memset(acc[:, 0, :], TINY)
                    e.memset(acc[:, 1, :], 0.0)
                    e.drain()
                passes(who, e, S)
                if who in ("pe", "act"):
                    e.wait_ge(S("params"), 16 * 6)
                hidden_general(who, e, S)
            return part

        def edge_layers_general():
            X, A, T = work[:, 0, :], work[:, 1, :], work[:, 2, :]
            own, other = ring[:, 0, :, :], ring[:, 1, :, HALF:HALF + D]
            dst_f = small[:, 0:J]

            def load_dst(e, S, g):
                e.dma_start(dst_cols[:, 0:J].rearrange("p (o j) -> p o j", o=1),
                            dst_pad[one(g), :].rearrange("o (p j) -> p o j", j=J)).then_inc(S("all_cols"), 16)
                e.wait_ge(S("all_cols"), g.times(16, 16))

            def clamp_dst(e, S, g):
                e.tensor_copy(dst_f, dst_cols[:, 0:J])
                e.drain()
                e.tensor_scalar(dst_f, dst_f, float(N - 1), None, ALU.min)
                e.drain()
                e.tensor_copy(dst_cols[:, J:2 * J], dst_f)

            def load_e0(e, S, g):
                e.dma_start(own[:, :, 0:HALF], e0_rows[one(g), :, :].rearrange("o p (j c) -> (o p) j c", j=J)).then_inc(S("all_e0"), 16)
                e.wait_ge(S("all_e0"), g.times(16, 16))

            def both_ends(e, S, g):
                e.tensor_tensor(own[:, :, HALF:3 * HALF], own[:, :, HALF:3 * HALF], other, ALU.add)

            def copy(bank, dst):
                return lambda e, S, g: e.tensor_copy(dst, bank[:, :])

            def few(bank, name):
                return lambda e, S, g: e.matmul(bank[:, :], lin[name][:, :], X, start=True, stop=True)

            def relu(bank, l):
                return lambda e, S, g: e.activation(A, bank[:, :], ACT.Relu, bias=bias(l, 1))

            def ew(bank, pair):
                def step(e, S, g):
                    for j in range(J):
                        e.matmul(bank[:, j * P:(j + 1) * P], A[:, j * P:(j + 1) * P], pair[:, :], start=True, stop=True)
                return step

            def by_edge(bank, c0):
                return lambda e, S, g: e.activation(own[:, :, c0:c0 + HALF], bank[:, :].rearrange("p (j c) -> p j c", j=J)[:, :, 0:HALF], ACT.Relu)

            def sums(e, S, g):
                e.tensor_copy(T, ps[6][:, :])
                e.drain()
                lo, hi = slice(0, HALF), slice(HALF, P)

                def add(c, d):
                    e.tensor_tensor(Z1[lo, d], Z1[lo, d], T[lo, c], ALU.add)
                    e.tensor_tensor(Z2[hi, d], Z2[hi, d], T[hi, c], ALU.add)
                serial(e, add)

            return relay([[
                ("act", take_sources), ("sync", take_destinations("all_dst0")), ("sync", load_dst), ("dve", clamp_dst),
                ("pool", all_gather("h", [(h_table, own[:, :, HALF:3 * HALF], idx_ring[:, 0, :]),
                                          (h_table, other, dst_cols[:, J:2 * J])])),
                ("sync", load_e0), ("dve", both_ends),
                ("pe", turn_rows(ps[0], own[:, :, 0:P])), ("dve", copy(ps[0], X)), ("pe", few(ps[1], "few0")), ("act", relu(ps[1], 0)),
                ("pe", ew(ps[2], ew1_pair)), ("act", by_edge(ps[2], 3 * HALF)),
                ("pe", turn_rows(ps[3], own[:, :, 2 * HALF:4 * HALF])), ("dve", copy(ps[3], X)), ("pe", few(ps[4], "few1")), ("act", relu(ps[4], 1)),
                ("pe", ew(ps[5], ew2_pair)), ("act", by_edge(ps[5], 4 * HALF)),
                ("pe", turn_rows(ps[6], own[:, :, 3 * HALF:5 * HALF])), ("dve", sums)]])

        ALL = "baton all_dst0 all_dst1 all_dst2 all_ea all_e0 all_cols".split()

        def gathers(e, S, i, table, dst, tag):
            s = i.off % RING
            wait(e, S("idx"), i)
            begin(e, S)
            for j in range(J):
                e.indirect_dma_start(out=dst[:, s, j, :], out_offset=None, in_=table,
                                     in_offset=bass.IndirectOffsetOnAxis(ap=idx_ring[:, s, j:j + 1], axis=0)
                                     ).then_inc(S(f"gather{tag}_{s}"), 16)

        def gathered(e, S, i, tag):
            wait(e, S(f"gather{tag}_{i.off % RING}"), i, 8, 64 - 8 * (i.off % RING))

        def first_indices(e, S):
            for g in range(RING):
                e.activation(idx_ring[:, g, :], src_idx[:, g, :], ACT.Copy).then_inc(S("idx"), 1)

        def next_indices(e, S, i):
            if i.base is not None or i.off + RING < NG:
                e.activation(idx_ring[:, i.off % RING, :].rearrange("p (o j) -> p o j", o=1),
                             src_idx[:, bass.ds(i.times(1, RING), 1), :], ACT.Copy).then_inc(S("idx"), 1)

        def make_onehot(e, i):
            g = bass.ds(i.times(1), 1)
            to = rel[:, g, :].rearrange("p o j -> p (o j)").rearrange("p (j o) -> p j o", o=1).broadcast_to([P, J, W])
            at = iota_w[:, :].rearrange("p (o w) -> p o w", o=1).broadcast_to([P, J, W])
            return e.tensor_tensor(onehot[:, i.off % RING, :, 0:W], to, at, ALU.is_equal)

        def window_start(e, i):
            return e.value_load(starts[0:1, bass.ds(i.times(1), 1)], min_val=0, max_val=N - 1)

        def edges_phase(layer, attr):
            ea = [work[:, s, 0:J * DE].rearrange("p (j c) -> p j c", j=J) for s in range(4)]
            eaT = [work[:, 4 + s, 0:2 * P] for s in range(2)]
            er = [ring[:, s, :, 2 * D:2 * D + HALF] for s in range(RING)]
            sums = [work[:, s, 256:256 + 4 * W].rearrange("p (k w) -> p k w", k=2) for s in range(4)]
            aggr = [work[:, s, 256 + 4 * W:256 + 5 * W] for s in range(4)]
            node = [work[:, 4 + s, 256:256 + P] for s in range(2)]

            def loads(e, S):
                for t, n in ((b1, "b1"), (gam, "gamma"), (bet, "beta")):
                    e.dma_start(t[:, :], a["L0_gnn_" + n][layer, :].rearrange("(h k) -> k h", k=P),
                                allow_slow_non_contiguous=True).then_inc(S("params"), 16)
                e.dma_start(b2[:, :], a["L0_gnn_b2"][layer, :].rearrange("(k o) -> k o", o=1)).then_inc(S("params"), 16)
                e.dma_start(W1[:, :], a["L0_gnn_W1"][layer, :, :]).then_inc(S("params"), 16)
                e.dma_start(W2[:, :, :], a["L0_gnn_W2"][layer, :, :].rearrange("(h k) m -> k h m", k=P)).then_inc(S("params"), 16)

            def sync(e, S):
                if attr:
                    def step(i):
                        if i.inside(NG):
                            wait(e, S("eaT"), i - 4)
                            begin(e, S)
                            s = i.off % 4
                            if i.base is None and i.off == NG - 1:
                                full = LAST // J
                                src = a["edge_attr_64"][(NG - 1) * GE:(NG - 1) * GE + full * J, :]
                                e.dma_start(ea[s][0:full, :, :], src.rearrange("(p j) c -> p j c", j=J)).then_inc(S(f"ea{s}"), 16)
                                e.dma_start(ea[s][full:full + 1, 0:LAST - full * J, :],
                                            a["edge_attr_64"][E - (LAST - full * J):E, :].rearrange("(o j) c -> o j c", o=1)).then_inc(S(f"ea{s}"), 16)
                            else:
                                src = a["edge_attr_64"][bass.ds(i.times(GE), GE), :]
                                e.dma_start(ea[s], src.rearrange("(p j) c -> p j c", j=J)).then_inc(S(f"ea{s}"), 16)
                        if (i - 4).inside(NG):
                            k = i - 4
                            wait(e, S("er"), k)
                            begin(e, S)
                            dst = e0_rows[bass.ds(k.times(1), 1), :, :].rearrange("o p c -> (o p) c")
                            e.dma_start(dst.rearrange("p (j c) -> p j c", j=J), er[k.off % RING]).then_inc(S(f"e0_out{k.off % RING}"), 16)
                    pipeline(e, NG, RING, RING, 4, step)
                    for s in range(RING):
                        e.wait_ge(S(f"e0_out{s}"), 16 * (NG // RING))

            def pool(e, S):
                def step(i):
                    wait(e, S("sums"), i - RING)
                    gathers(e, S, i, msg_table, msg, layer)
                pipeline(e, NG, RING, RING, 0, step)

            def act(e, S):
                first_indices(e, S)
                e.wait_ge(S("params"), 16 * 6)
                hidden_columns(e, S)
                e.wait_ge(S("hid"), NCH)

                def step(i):
                    if (i - 4).inside(NG):
                        k = i - 4
                        w = window_start(e, k)
                        wait(e, S("Wnode"), k)
                        wait(e, S("hid_w"), k - 1)
                        for h in range(2):
                            ins = e.activation(hid[:, h, bass.ds(w, W)], ps[2 + k.off % 2][:, 256 + h * P:256 + h * P + W],
                                               ACT.Identity, bias=b1[:, h:h + 1])
                        ins.then_inc(S("hid_w"), 1)
                    if i.inside(NG):
                        gathered(e, S, i, layer)
                        e.activation(ex[:, i.off % RING, :, :], msg[:, i.off % RING, :, :], ACT.Exp,
                                     bias=negc[:, :]).then_inc(S("exp"), 1)
                        next_indices(e, S, i)
                    if attr and (i - 1).inside(NG):
                        k = i - 1
                        wait(e, S("ea_turned"), k)
                        wait(e, S("e0"), k - 2)
                        e.activation(eaT[k.off % 2], ps[2 + k.off % 2][:, 0:2 * P], ACT.Copy).then_inc(S("eaT"), 1)
                pipeline(e, NG, RING, RING, 4, step)

            def pe(e, S):
                def without_edges(i):
                    wait(e, S("hid"), i - 2)
                    for h in range(2):
                        ins = e.matmul(ps[i.off % 2][:, h * 256:h * 256 + CH], W1[:, h * P:(h + 1) * P], xT[:, cols(i)],
                                       start=True, stop=True)
                    ins.then_inc(S("W1"), 1)
                e.wait_ge(S("params"), 16 * 6)
                pipeline(e, NCH, 2, 2, 0, without_edges)
                e.wait_ge(S("hid"), NCH)

                def step(i):
                    if i.inside(NG):
                        s, bank = i.off % RING, ps[i.off % 2]
                        if attr:
                            last = i.base is None and i.off == NG - 1
                            wait(e, S(f"ea{i.off % 4}"), i, 4, 16 - 4 * (i.off % 4) + 16 * last)
                            wait(e, S("eaT"), i - 2)
                            wait(e, S("hid_w"), i - 4)
                            for h in range(J // 2):
                                pair = ea[i.off % 4][:, 2 * h:2 * h + 2, :].rearrange("p j c -> p (j c)")
                                ins = e.transpose(ps[2 + i.off % 2][:, h * P:(h + 1) * P], pair, ident[:, :])
                            ins.then_inc(S("ea_turned"), 1)
                    if attr and (i - 1).inside(NG):
                        k = i - 1
                        wait(e, S("eaT"), k)
                        wait(e, S("er"), k - 2)
                        for h in range(J // 2):
                            ins = e.matmul(ps[4 + k.off % 2][:, h * P:(h + 1) * P], eaT[k.off % 2][:, h * P:(h + 1) * P],
                                           ew0_pair[:, :], start=True, stop=True)
                        ins.then_inc(S("e0"), 1)
                    if (i - 3).inside(NG):
                        k = i - 3
                        wait(e, S("node"), k)
                        wait(e, S("hid_w"), k - 2)
                        for h in range(2):
                            ins = e.matmul(ps[2 + k.off % 2][:, 256 + h * P:256 + (h + 1) * P], W1[:, h * P:(h + 1) * P],
                                           node[k.off % 2], start=True, stop=True)
                        ins.then_inc(S("Wnode"), 1)
                    if attr and (i - 2).inside(NG):
                        k = i - 2
                        wait(e, S("er"), k)
                        wait(e, S("agg0"), k - 2)
                        for j in range(J):
                            ins = e.matmul(ps[6 + k.off % 2][0:HALF, 0:P], er[k.off % RING][:, j, :],
                                           onehot[:, k.off % RING, j, :], start=(j == 0), stop=(j == J - 1))
                        ins.then_inc(S("e0_sums"), 1)
                    if i.inside(NG):
                        wait(e, S("mexp"), i)
                        wait(e, S("acc"), i - 2)
                        for k, rows in enumerate((ex, msg)):
                            for j in range(J):
                                ins = e.matmul(bank[:, k * P:(k + 1) * P], rows[:, s, j, :], onehot[:, s, j, :],
                                               start=(j == 0), stop=(j == J - 1))
                        ins.then_inc(S("sums"), 1)
                pipeline(e, NG, RING, RING, 3, step)

            def dve(e, S):
                for t in sums:
                    e.memset(t[:, 0, :], TINY).then_inc(S("zero"), 1)
                    e.memset(t[:, 1, :], 0.0).then_inc(S("zero"), 1)
                for t in node:
                    e.memset(t, 0.0).then_inc(S("zero"), 1)
                e.wait_ge(S("zero"), 10)

                def step(i):
                    if i.inside(NG):
                        s = i.off % RING
                        wait(e, S("sums"), i - RING)
                        if attr:
                            wait(e, S("e0_sums"), i - RING)
                        make_onehot(e, i).then_inc(S("onehot"), 1)
                    if (i - 2).inside(NG):
                        k = i - 2
                        wait(e, S("acc"), k)
                        e.reciprocal(aggr[k.off % 4], sums[k.off % 4][:, 0, 0:W]).then_inc(S("quot"), 1)
                    if i.inside(NG):
                        wait(e, S("exp"), i)
                        e.scalar_tensor_tensor(out=msg[:, s, :, :], in0=msg[:, s, :, :], scalar=EPS_MSG,
                                               in1=ex[:, s, :, :], op0=ALU.add, op1=ALU.mult).then_inc(S("mexp"), 1)
                    if (i - 2).inside(NG):
                        t = aggr[k.off % 4]
                        wait(e, S("quot"), k, 2, 1)
                        e.tensor_tensor(t, t, sums[k.off % 4][:, 1, 0:W], ALU.mult).then_inc(S("quot"), 1)
                    if attr and (i - 1).inside(NG):
                        k = i - 1
                        wait(e, S("e0"), k)
                        s = k.off % RING
                        wait(e, S(f"e0_out{s}"), k, 2, -2 * s)
                        e.tensor_scalar(er[s], ps[4 + k.off % 2][:, 0:J * HALF].rearrange("p (j c) -> p j c", j=J), 0.0, None,
                                        ALU.max).then_inc(S("er"), 1)
                    if (i - 1).inside(NG):
                        k = i - 1
                        by = e.value_load(shifts[0:1, bass.ds(k.times(1), 1)], min_val=0, max_val=W)
                        wait(e, S("sums"), k)
                        wait(e, S("acc"), k - 1)
                        new = ps[k.off % 2][:, 0:2 * P].rearrange("p (k w) -> p k w", k=2)[:, :, 0:W]
                        e.tensor_tensor(sums[k.off % 4][:, :, 0:W], sums[(k.off - 1) % 4][:, :, bass.ds(by, W)], new,
                                        ALU.add).then_inc(S("acc"), 1)
                    if (i - 2).inside(NG):
                        k = i - 2
                        w = window_start(e, k)
                        wait(e, S("quot"), k, 2, 2)
                        wait(e, S("Wnode"), k - 2)
                        e.tensor_tensor(node[k.off % 2][:, 0:W], aggr[k.off % 4], xT_all[:, bass.ds(w, W)],
                                        ALU.add).then_inc(S("node"), 1)
                    if attr and (i - 3).inside(NG):
                        k = i - 3
                        w = window_start(e, k)
                        wait(e, S("e0_sums"), k)
                        wait(e, S("agg0"), k - 1)
                        place = Z0[0:HALF, bass.ds(w, W)]
                        e.tensor_tensor(place, place, ps[6 + k.off % 2][0:HALF, 0:W], ALU.add).then_inc(S("agg0"), 1)
                pipeline(e, NG, RING, 2 * RING if attr else RING, 3 if attr else 2, step)

            names = ["params", "W1", "hid", "quot", "node", "Wnode", "hid_w", "issued", "eaT", "er", "exp", "ea_turned", "e0", "agg0", "e0_sums", "mexp", "acc", "sums", "zero",
                     "onehot", "idx"] + [f"{n}{s}" for n in ("e0_out",) for s in range(RING)] + [f"ea{s}" for s in range(4)]
            parts = either(0, edges_general(layer, attr), dict(sync=sync, pool=pool, act=act, pe=pe, dve=dve))
            edges_sync = parts["sync"]

            def load_and_sync(e, S):
                loads(e, S)
                edges_sync(e, S)
                e.wait_ge(S("params"), 16 * 6)
            parts["sync"] = load_and_sync
            return ("edges", names + ALL, parts)


        def nodes_phase(last):
            hr = [work[:, b, 0:2 * CH].rearrange("p (h n) -> p h n", h=2) for b in range(4)]
            xc = [work[:, 4 + b // 2, b % 2 * 256:b % 2 * 256 + CH] for b in range(4)]
            hrow = [ring[0:TILE, b, 0, 0:2 * D].rearrange("p (k d) -> p k d", k=2) for b in range(4)]

            def pool(e, S):
                def step(i):
                    wait(e, S("x_new"), i)
                    begin(e, S)
                    e.tensor_copy(xT[:, cols(i)], xc[i.off % 4]).then_inc(S("x_kept"), 1)
                pipeline(e, NCH, 4, 4, 0, step)

            def dve(e, S):
                def stats(k):
                    for h in range(2):
                        if k.base is None:
                            st = stat[:, h, k.off, :]
                        else:
                            st = stat[:, h, bass.ds(k.times(1), 1), :].rearrange("p o s -> p (o s)")
                        e.bn_stats(st, hid[:, h, cols(k)]).then_inc(S("stats"), 1)
                pipeline(e, NCH, 2, 2, 0, stats)
                e.wait_ge(S("stats"), 2 * NCH)
                v = [0]

                def then(ins):
                    v[0] += 1
                    ins.then_inc(S("scale"), 1)
                    e.wait_ge(S("scale"), v[0])
                for h in range(2):
                    then(e.bn_aggr(mv[:, h, 0:2], stat[:, h, :, :].rearrange("p c s -> p (c s)")))
                mean, var = (mv[:, 0:2, k] for k in range(2))
                then(e.tensor_scalar(sc[:, 0:2], var, EPS, None, ALU.add))
                e.sem_inc(S("var"), 1)
                e.wait_ge(S("root"), 1)
                then(e.reciprocal(sc[:, 0:2], sc[:, 0:2]))
                then(e.tensor_tensor(sc[:, 0:2], sc[:, 0:2], gam[:, :], ALU.mult))
                then(e.tensor_tensor(sh[:, 0:2], mean, sc[:, 0:2], ALU.mult))
                then(e.tensor_tensor(sh[:, 0:2], bet[:, :], sh[:, 0:2], ALU.subtract))
                e.sem_inc(S("norm"), 1)

                def out_rows(i):
                    if i.inside(NCH):
                        b = xc[i.off % 4]
                        wait(e, S("W2"), i)
                        wait(e, S("x_kept"), i - 4)
                        wait(e, S("turn"), i - 4)
                        wait(e, S("cmax"), i - 4)
                        e.tensor_scalar(b, ps[i.off % 4][:, 0:CH], b2[:, :], 0.0, ALU.add, ALU.max).then_inc(S("x_new"), 1)
                    if (i - 1).inside(NCH):
                        k = i - 1
                        wait(e, S("x_new"), k)
                        c = slice(k.off, k.off + 1) if k.base is None else bass.ds(k.times(1), 1)
                        e.tensor_reduce(cmax[:, c], xc[k.off % 4], AX, ALU.max).then_inc(S("cmax"), 1)
                pipeline(e, NCH, 4, 8, 1, out_rows)
                e.wait_ge(S("cmax"), NCH)
                if not last:
                    shift_dve(e, S)

            def act(e, S):
                e.wait_ge(S("var"), 1)
                e.activation(sc[:, 0:2], sc[:, 0:2], ACT.Sqrt).then_inc(S("root"), 1)
                e.wait_ge(S("norm"), 1)

                def out_rows(i):
                    if i.inside(NCH):
                        wait(e, S("W2"), i - 4)
                        for h in range(2):
                            ins = e.activation(hr[i.off % 4][:, h, :], hid[:, h, cols(i)], ACT.Relu,
                                               bias=sh[:, h:h + 1], scale=sc[:, h:h + 1])
                        ins.then_inc(S("hr"), 1)
                    if (i - 2).inside(NCH):
                        k = i - 2
                        wait(e, S("turn"), k)
                        wait(e, S(TABLE[k.off % 4]), k, 4, -4 * (k.off % 4))
                        e.activation(hrow[k.off % 4], ps[4 + k.off % 4][0:TILE, 0:2 * D].rearrange("p (k d) -> p k d", k=2),
                                     ACT.Copy).then_inc(S("rows"), 1)
                pipeline(e, NCH, 4, 8, 2, out_rows)

            def pe(e, S):
                def out_rows(i):
                    if i.inside(NCH):
                        wait(e, S("hr"), i)
                        wait(e, S("x_new"), i - 4)
                        for h in range(2):
                            ins = e.matmul(ps[i.off % 4][:, 0:CH], W2[:, h, :], hr[i.off % 4][:, h, :],
                                           start=(h == 0), stop=(h == 1))
                        ins.then_inc(S("W2"), 1)
                    if (i - 1).inside(NCH):
                        k = i - 1
                        wait(e, S("x_new"), k)
                        wait(e, S("rows"), k - 4)
                        for t in range(2):
                            ins = e.transpose(ps[4 + k.off % 4][0:TILE, t * D:(t + 1) * D],
                                              xc[k.off % 4][:, t * TILE:(t + 1) * TILE], ident[:, :])
                        ins.then_inc(S("turn"), 1)
                pipeline(e, NCH, 4, 8, 1, out_rows)
                if not last:
                    shift_pe(e, S)

            def sync(e, S):
                def step(i):
                    wait(e, S("rows"), i)
                    begin(e, S)
                    e.dma_start(rows_of(msg_table, i), hrow[i.off % 4]).then_inc(S(TABLE[i.off % 4]), 16)
                pipeline(e, NCH, 4, 4, 0, step)
                stores(e, S, TABLE, NCH)

            names = "issued x_new x_kept stats scale var root norm W2 turn cmax hr rows".split() + TABLE + SHIFT
            return ("nodes", names, dict(sync=sync, pool=pool, act=act, pe=pe, dve=dve))

        for layer in range(L):
            phases.append(edges_phase(layer, layer == 0))
            phases.append(nodes_phase(layer == L - 1))
        phases.append(norm_phase(False))

        def hidden_phase():
            hc = [work[:, 5 * (b // 2), b % 2 * 256:b % 2 * 256 + CH] for b in range(4)]
            x1 = [work[:, 1, b * 256:b * 256 + CH] for b in range(2)]
            hrow = rowring(2)
            low = [work[0:TILE, 4, b * 256:(b + 1) * 256].rearrange("p (k d) -> p k d", k=2) for b in range(2)]
            part = [[ring[0:TILE, b * 3 + k, 0, 0:D].bitcast(BF16).rearrange("p (k d) -> p k d", k=2) for k in range(3)]
                    for b in range(2)]
            zero = ring[0:W, 6, 0, 0:3 * HALF].bitcast(BF16)

            def pe(e, S):
                def step(i):
                    if i.inside(NCH):
                        wait(e, S("h0"), i - 2)
                        wait(e, S("h0c"), i - 2)
                        e.matmul(ps[i.off % 2][:, 0:CH], lin["nw0"][:, :], xT[:, cols(i)], start=True, stop=True).then_inc(S("nw0"), 1)
                    if (i - 1).inside(NCH):
                        k = i - 1
                        wait(e, S("h0"), k)
                        wait(e, S("h0c"), k)
                        wait(e, S("y"), k - 2)
                        e.matmul(ps[2 + k.off % 2][:, 0:CH], lin["fnw0"][:, :], Z0[:, cols(k)], start=True, stop=True).then_inc(S("fnw0"), 1)
                    if (i - 2).inside(NCH):
                        k = i - 2
                        wait(e, S("x1"), k)
                        wait(e, S("h1"), k - 2)
                        wait(e, S("h1c"), k - 2)
                        e.matmul(ps[4 + k.off % 2][:, 0:CH], nw1_pair[:, :], x1[k.off % 2], start=True, stop=True).then_inc(S("nw1"), 1)
                    if (i - 3).inside(NCH):
                        k = i - 3
                        wait(e, S("h1"), k)
                        wait(e, S("h1c"), k)
                        wait(e, S("rows"), k - 2)
                        for t in range(2):
                            ins = e.transpose(ps[6 + k.off % 2][0:TILE, t * D:(t + 1) * D], hc[k.off % 4][:, t * TILE:(t + 1) * TILE],
                                              ident[:, :])
                        ins.then_inc(S("turn"), 1)
                pipeline(e, NCH, 4, 8, 3, step)

            def act(e, S):
                def step(i):
                    if i.inside(NCH):
                        wait(e, S("nw0"), i)
                        e.activation(Z0[HALF:P, cols(i)], ps[i.off % 2][HALF:P, 0:CH], ACT.Relu).then_inc(S("h0"), 1)
                    if (i - 1).inside(NCH):
                        k = i - 1
                        wait(e, S("fnw0"), k)
                        wait(e, S("nw1"), k - 2)
                        e.activation(x1[k.off % 2], ps[2 + k.off % 2][:, 0:CH], ACT.Relu, bias=bias(0, 0)).then_inc(S("y"), 1)
                    if (i - 2).inside(NCH):
                        k = i - 2
                        wait(e, S("nw1"), k)
                        e.activation(Z1[HALF:P, cols(k)], ps[4 + k.off % 2][HALF:P, 0:CH], ACT.Relu).then_inc(S("h1"), 1)
                    if (i - 3).inside(NCH):
                        k = i - 3
                        wait(e, S("turn"), k)
                        wait(e, S(TABLE[k.off % 4]), k, 4, -4 * (k.off % 4))
                        wait(e, S("high"), k - 4, 2)
                        e.activation(hrow[k.off % 4], ps[6 + k.off % 2][0:TILE, 0:2 * D].rearrange("p (k d) -> p k d", k=2),
                                     ACT.Copy).then_inc(S("rows"), 1)
                pipeline(e, NCH, 4, 8, 3, step)

            def dve(e, S):
                e.memset(zero, 0.0).then_inc(S("zero"), 1)
                e.memset(Z1[0:HALF, :], 0.0).then_inc(S("z"), 1)
                e.memset(Z2[:, :], 0.0).then_inc(S("z"), 1)
                e.wait_ge(S("z"), 2)

                def step(i):
                    if i.inside(NCH):
                        wait(e, S("nw0"), i)
                        wait(e, S("turn"), i - 4)
                        e.tensor_scalar(hc[i.off % 4][0:HALF, :], ps[i.off % 2][0:HALF, 0:CH], 0.0, None, ALU.max).then_inc(S("h0c"), 1)
                    if (i - 1).inside(NCH):
                        k = i - 1
                        wait(e, S("y"), k)
                        e.tensor_scalar(x1[k.off % 2], x1[k.off % 2], bias(0, 2), bias(0, 3), ALU.mult, ALU.add).then_inc(S("x1"), 1)
                    if (i - 2).inside(NCH):
                        k = i - 2
                        wait(e, S("nw1"), k)
                        e.tensor_scalar(hc[k.off % 4][HALF:P, :], ps[4 + k.off % 2][0:HALF, 0:CH], 0.0, None, ALU.max).then_inc(S("h1c"), 1)
                    if (i - 4).inside(NCH):
                        k = i - 4
                        b = k.off % 2
                        wait(e, S("rows"), k)
                        wait(e, S(f"hp{b}"), k, 24, -24 * b)
                        wait(e, S("low"), k - 2)
                        e.tensor_copy(part[b][0], hrow[k.off % 4]).then_inc(S("high"), 1)
                        wait(e, S("high"), k, 2, 1)
                        e.tensor_tensor(low[b], hrow[k.off % 4], part[b][0], ALU.subtract).then_inc(S("high"), 1)
                pipeline(e, NCH, 4, 8, 4, step)

            def pool(e, S):
                def step(i):
                    b = i.off % 2
                    wait(e, S("high"), i, 2)
                    wait(e, S(f"hp{b}"), i, 24, -24 * b)
                    begin(e, S)
                    e.tensor_copy(part[b][1], low[b]).then_inc(S("mid"), 1)
                    wait(e, S("mid"), i)
                    begin(e, S)
                    e.tensor_tensor(part[b][2], low[b], part[b][1], ALU.subtract).then_inc(S("low"), 1)
                pipeline(e, NCH, 4, 8, 0, step)

            def sync(e, S):
                e.wait_ge(S("zero"), 1)
                e.dma_start(h_parts[:, N:NP, :].rearrange("k r d -> r k d"), zero.rearrange("r (k d) -> r k d", k=3)).then_inc(S("zeros"), 16)

                def step(i):
                    if i.inside(NCH):
                        wait(e, S("rows"), i)
                        begin(e, S)
                        e.dma_start(rows_of(h_table, i), hrow[i.off % 4]).then_inc(S(TABLE[i.off % 4]), 16)
                    if (i - 2).inside(NCH):
                        k = i - 2
                        b = k.off % 2
                        wait(e, S("low"), k)
                        begin(e, S)
                        for q in range(3):
                            e.dma_start(rows_of(h_parts[q, 0:N, :], k), part[b][q]).then_inc(S(f"hp{b}"), 16)
                pipeline(e, NCH, 4, 8, 2, step)
                stores(e, S, TABLE, NCH)
                for b in range(2):
                    e.wait_ge(S(f"hp{b}"), 48 * len(range(b, NCH, 2)))
                e.wait_ge(S("zeros"), 16)

            names = "issued nw0 fnw0 nw1 turn h0 h0c y h1 h1c x1 rows high mid low zero zeros z hp0 hp1".split() + TABLE
            return ("hidden", names, dict(sync=sync, pool=pool, act=act, pe=pe, dve=dve))

        def edge_layers_phase():
            X1, X2 = ([work[:, b, :] for b in range(2)], [work[:, 2 + b, :] for b in range(2)])
            A, C = work[:, 4, :], work[:, 5, :]
            rows = ring[:, :, :, HALF:HALF + D]
            TAG = "h"

            def sync(e, S):
                def step(i):
                    if i.inside(NG):
                        s = i.off % RING
                        wait(e, S("turn2"), i - RING)
                        begin(e, S)
                        wait(e, S("one_hotT"), i - 4)
                        begin(e, S)
                        at = bass.ds(i.times(1), 1)
                        src = rel_rows[at, :, :].rearrange("o j p -> o (j p)").broadcast_to([3 * W, GE])
                        e.dma_start(relb[:, i.off % 4, :], src).then_inc(S(f"rel{i.off % 4}"), 16)
                        w = e.value_load(starts[0:1, at], min_val=0, max_val=N - 1)
                        for q in range(3):
                            e.dma_start(window[q * W:(q + 1) * W, s, :], h_parts[q, bass.ds(w, W), :]).then_inc(S(f"window{s}"), 16)
                        e.dma_start(ring[:, s, :, 0:HALF],
                                    e0_rows[at, :, :].rearrange("o p (j c) -> (o p) j c", j=J)).then_inc(S(f"e0{s}"), 16)
                pipeline(e, NG, RING, RING, 0, step)

            def pool(e, S):
                def step(i):
                    wait(e, S("turn2"), i - RING)
                    gathers(e, S, i, h_table, rows, TAG)
                pipeline(e, NG, RING, RING, 0, step)

            def turn(e, S, i, bank, c0, half, h0):
                s = i.off % RING
                for j in range(J):
                    e.matmul(bank[:, j * P:(j + 1) * P], ring[:, s, j, c0:c0 + P], ident[:, :], is_transpose=True,
                             start=(j == 0), stop=False, skip_group_check=True)
                return e.matmul(bank[half, :], window[:, s, h0:h0 + HALF], onehotT[:, s % 4, :], start=False, stop=True,
                                skip_group_check=True)

            def pe(e, S):
                def step(i):
                    if i.inside(NG):
                        s = i.off % RING
                        gathered(e, S, i, TAG)
                        wait(e, S(f"e0{s}"), i, 2, 16 - 2 * s)
                        wait(e, S(f"window{s}"), i, 6, 48 - 6 * s)
                        wait(e, S("one_hotT"), i)
                        wait(e, S("X1"), i - 1)
                        turn(e, S, i, ps[0], 0, slice(HALF, P), 0).then_inc(S("turn1"), 1)
                    if (i - 1).inside(NG):
                        k = i - 1
                        wait(e, S("X1"), k)
                        wait(e, S("A"), k - 1)
                        e.matmul(ps[1][:, :], lin["few0"][:, :], X1[k.off % 2], start=True, stop=True).then_inc(S("few0"), 1)
                    if (i - 2).inside(NG):
                        k = i - 2
                        wait(e, S("A"), k)
                        wait(e, S("e1"), k - 1)
                        for j in range(J):
                            ins = e.matmul(ps[2][:, j * P:(j + 1) * P], A[:, j * P:(j + 1) * P], ew1_pair[:, :], start=True, stop=True)
                        ins.then_inc(S("ew1"), 1)
                    if (i - 3).inside(NG):
                        k = i - 3
                        wait(e, S("e1"), k)
                        wait(e, S("X2"), k - 1)
                        turn(e, S, k, ps[3], 2 * HALF, slice(0, HALF), HALF).then_inc(S("turn2"), 1)
                    if (i - 4).inside(NG):
                        k = i - 4
                        wait(e, S("X2"), k)
                        wait(e, S("C"), k - 1)
                        e.matmul(ps[4][:, :], lin["few1"][:, :], X2[k.off % 2], start=True, stop=True).then_inc(S("few1"), 1)
                    if (i - 5).inside(NG):
                        k = i - 5
                        wait(e, S("C"), k)
                        wait(e, S("e2"), k - 1)
                        for j in range(J):
                            ins = e.matmul(ps[5][:, j * P:(j + 1) * P], C[:, j * P:(j + 1) * P], ew2_pair[:, :], start=True, stop=True)
                        ins.then_inc(S("ew2"), 1)
                    if (i - 6).inside(NG):
                        k = i - 6
                        s = k.off % RING
                        wait(e, S("e2"), k)
                        wait(e, S("agg"), k - 2, 2)
                        wait(e, S("onehot"), k)
                        for j in range(J):
                            ins = e.matmul(ps[6 + k.off % 2][:, 0:P], ring[:, s, j, 3 * HALF:5 * HALF], onehot[:, s, j, :],
                                           start=(j == 0), stop=(j == J - 1))
                        ins.then_inc(S("sums"), 1)
                pipeline(e, NG, RING, RING, 6, step)

            def act(e, S):
                first_indices(e, S)

                def by_edge(k, bank, c0, name):
                    return e.activation(ring[:, k.off % RING, :, c0:c0 + HALF],
                                        bank[:, :].rearrange("p (j c) -> p j c", j=J)[:, :, 0:HALF], ACT.Relu).then_inc(S(name), 1)

                def step(i):
                    if i.inside(NG):
                        gathered(e, S, i, TAG)
                        next_indices(e, S, i)
                    if (i - 1).inside(NG):
                        k = i - 1
                        wait(e, S("few0"), k)
                        wait(e, S("ew1"), k - 1)
                        e.activation(A, ps[1][:, :], ACT.Relu, bias=bias(0, 1)).then_inc(S("A"), 1)
                    if (i - 2).inside(NG):
                        wait(e, S("ew1"), i - 2)
                        by_edge(i - 2, ps[2], 3 * HALF, "e1")
                    if (i - 4).inside(NG):
                        k = i - 4
                        wait(e, S("few1"), k)
                        wait(e, S("ew2"), k - 1)
                        e.activation(C, ps[4][:, :], ACT.Relu, bias=bias(1, 1)).then_inc(S("C"), 1)
                    if (i - 5).inside(NG):
                        wait(e, S("ew2"), i - 5)
                        by_edge(i - 5, ps[5], 4 * HALF, "e2")
                pipeline(e, NG, RING, RING, 5, step)

            def dve(e, S):
                def hots(i):
                    wait(e, S("sums"), i - RING)
                    make_onehot(e, i).then_inc(S("onehot"), 1)
                    wait(e, S(f"rel{i.off % 4}"), i, 4, 16 - 4 * (i.off % 4))
                    wait(e, S("turn2"), i - 4)
                    e.tensor_scalar(onehotT[:, i.off % 4, :], relb[:, i.off % 4, :], iota_p[0:3 * W, :], None,
                                    ALU.is_equal).then_inc(S("one_hotT"), 1)

                def step(i):
                    if i.base is None and i.off == 0:
                        hots(i)
                    if (i - -1).inside(NG):
                        hots(i - -1)
                    if i.inside(NG):
                        wait(e, S("turn1"), i)
                        wait(e, S("few0"), i - 2)
                        e.tensor_copy(X1[i.off % 2], ps[0][:, :]).then_inc(S("X1"), 1)
                    if (i - 3).inside(NG):
                        k = i - 3
                        wait(e, S("turn2"), k)
                        wait(e, S("few1"), k - 2)
                        e.tensor_copy(X2[k.off % 2], ps[3][:, :]).then_inc(S("X2"), 1)
                    if (i - 7).inside(NG):
                        k = i - 7
                        w = window_start(e, k)
                        wait(e, S("sums"), k)
                        wait(e, S("agg"), k - 1, 2)
                        for half, Z in ((slice(0, HALF), Z1), (slice(HALF, P), Z2)):
                            place = Z[half, bass.ds(w, W)]
                            e.tensor_tensor(place, place, ps[6 + k.off % 2][half, 0:W], ALU.add).then_inc(S("agg"), 1)
                pipeline(e, NG, RING, RING, 7, step)

            names = ["issued", "idx", "sums", "one_hotT", "onehot", "X1", "X2", "turn1", "turn2", "few0", "few1", "A", "C",
                     "ew1", "ew2", "e1", "e2", "agg"] + [f"{n}{s}" for n in ("window", "e0") for s in range(RING)] + \
                    [f"rel{s}" for s in range(4)]
            return ("edge layers", names + ALL,
                    either(1, edge_layers_general(), dict(sync=sync, pool=pool, act=act, pe=pe, dve=dve)))

        def output_phase():
            y = [work[:, b, 0:CH] for b in range(2)]
            z = [work[:, b, 256:256 + CH] for b in range(2)]
            xm = rowring(2)
            orow = rowring(4)
            MID = ["mid0", "mid1", "mid2", "mid3"]

            def pe(e, S):
                def step(i):
                    if i.inside(NCH):
                        wait(e, S("y"), i - 2)
                        e.matmul(ps[i.off % 2][:, 0:CH], lin["fnw1"][:, :], Z1[:, cols(i)], start=True, stop=True).then_inc(S("fnw1"), 1)
                    if (i - 1).inside(NCH):
                        k = i - 1
                        wait(e, S("x2"), k)
                        wait(e, S("h2"), k - 2)
                        e.matmul(ps[2 + k.off % 2][0:HALF, 0:CH], lin["nw2"][:, :], y[k.off % 2], start=True, stop=True).then_inc(S("nw2"), 1)
                    if (i - 2).inside(NCH):
                        k = i - 2
                        wait(e, S("h2"), k)
                        wait(e, S("z"), k - 2)
                        e.matmul(ps[4 + k.off % 2][:, 0:CH], lin["fnw2"][:, :], Z2[:, cols(k)], start=True, stop=True).then_inc(S("fnw2"), 1)
                    if (i - 3).inside(NCH):
                        k = i - 3
                        wait(e, S("x3"), k)
                        wait(e, S("out"), k - 2)
                        for t in range(2):
                            ins = e.transpose(ps[6 + k.off % 2][0:TILE, t * D:(t + 1) * D], z[k.off % 2][:, t * TILE:(t + 1) * TILE],
                                              ident[:, :])
                        ins.then_inc(S("turn"), 1)
                pipeline(e, NCH, 4, 8, 3, step)

            def act(e, S):
                def step(i):
                    if i.inside(NCH):
                        wait(e, S("fnw1"), i)
                        wait(e, S("nw2"), i - 2)
                        e.activation(y[i.off % 2], ps[i.off % 2][:, 0:CH], ACT.Relu, bias=bias(1, 0)).then_inc(S("y"), 1)
                    if (i - 1).inside(NCH):
                        k = i - 1
                        wait(e, S("nw2"), k)
                        e.activation(Z2[0:HALF, cols(k)], ps[2 + k.off % 2][0:HALF, 0:CH], ACT.Relu).then_inc(S("h2"), 1)
                    if (i - 2).inside(NCH):
                        k = i - 2
                        wait(e, S("fnw2"), k)
                        wait(e, S("turn"), k - 2)
                        e.activation(z[k.off % 2], ps[4 + k.off % 2][:, 0:CH], ACT.Relu, bias=bias(2, 0)).then_inc(S("z"), 1)
                pipeline(e, NCH, 4, 4, 2, step)

            def dve(e, S):
                def step(i):
                    if i.inside(NCH):
                        wait(e, S("y"), i)
                        e.tensor_scalar(y[i.off % 2], y[i.off % 2], bias(1, 2), bias(1, 3), ALU.mult, ALU.add).then_inc(S("x2"), 1)
                    if (i - 2).inside(NCH):
                        k = i - 2
                        wait(e, S("z"), k)
                        e.tensor_scalar(z[k.off % 2], z[k.off % 2], bias(2, 2), bias(2, 3), ALU.mult, ALU.add).then_inc(S("x3"), 1)
                    if (i - 3).inside(NCH):
                        k = i - 3
                        b = k.off % 4
                        wait(e, S("turn"), k)
                        wait(e, S(MID[b]), k, 4, 16 - 4 * b)
                        wait(e, S(TABLE[b]), k, 4, -4 * b)
                        e.tensor_tensor(orow[b], xm[b], ps[6 + k.off % 2][0:TILE, 0:2 * D].rearrange("p (k d) -> p k d", k=2),
                                        ALU.add).then_inc(S("out"), 1)
                pipeline(e, NCH, 4, 8, 3, step)

            def sync(e, S):
                def step(i):
                    if i.inside(NCH):
                        wait(e, S("out"), i - 4)
                        begin(e, S)
                        e.dma_start(xm[i.off % 4], rows_of(x_mid, i)).then_inc(S(MID[i.off % 4]), 16)
                    if (i - 4).inside(NCH):
                        k = i - 4
                        wait(e, S("out"), k)
                        begin(e, S)
                        e.dma_start(rows_of(out, k), orow[k.off % 4]).then_inc(S(TABLE[k.off % 4]), 16)
                pipeline(e, NCH, 4, 4, 4, step)
                stores(e, S, TABLE, NCH)

            names = "issued fnw1 nw2 fnw2 turn y h2 z x2 x3 out".split() + TABLE + MID
            return ("output", names, dict(sync=sync, act=act, pe=pe, dve=dve))

        phases += [hidden_phase(), edge_layers_phase(), output_phase()]

        bar = sem("bar")
        shared = [sem(f"phase_sem{k}") for k in range(max(len(used) for _, used, _ in phases))]
        gather_sems = {}

        def names_of(used):
            def S(name):
                if name.startswith("gather"):
                    if name not in gather_sems:
                        gather_sems[name] = sem(name)
                    return gather_sems[name]
                return shared[used.index(name)]
            return S

        block = ctx.enter_context(nc.Block())

        def program(e, who):
            met = [0]

            def meet():
                met[0] += 1
                e.drain()
                e.sem_inc(bar, 1)
                e.wait_ge(bar, 5 * met[0])
                e.drain()

            for name, used, parts in phases:
                S = names_of(used)
                if who in parts:
                    parts[who](e, S)
                meet()
                if who == "sync":
                    for n in used:
                        e.sem_clear(S(n))
                meet()

        @block.sync
        def _(e):
            program(e, "sync")

        @block.gpsimd
        def _(e):
            program(e, "pool")

        @block.scalar
        def _(e):
            program(e, "act")

        @block.tensor
        def _(e):
            program(e, "pe")

        @block.vector
        def _(e):
            program(e, "dve")


_OUT = (N, D)


def kernel(**inputs):
    import numpy as np
    import concourse.bacc as bacc
    from concourse.bass_utils import run_bass_kernel_spmd
    nc = bacc.Bacc("TRN2", target_bir_lowering=False, num_devices=1)
    arrays, a = {}, {}
    for name, v in inputs.items():
        v = np.ascontiguousarray(v)
        arrays["in_" + name] = v
        a[name] = nc.dram_tensor("in_" + name, v.shape, mybir.dt.from_np(v.dtype), kind="ExternalInput").ap()
    out = nc.dram_tensor("out_nodes", _OUT, F32, kind="ExternalOutput").ap()
    gnn_kernel(nc, a, out)
    r = run_bass_kernel_spmd(nc, [arrays], core_ids=[0])
    return r.results[0]["out_nodes"]
```

```python
from contextlib import ExitStack

import concourse.bass as bass
from concourse import mybir

F32, I32, BF16 = mybir.dt.float32, mybir.dt.int32, mybir.dt.bfloat16
ALU = mybir.AluOpType
ACT = mybir.ActivationFunctionType
AX = mybir.AxisListType.X

N, E, D, DE, HID, HALF = 6250, 106250, 128, 64, 256, 64
ROW = D + HALF
L = 3
P = 128
TILE = 125
CH = 250
NCH = N // CH
J = 4
GE = P * J
NG = -(-E // GE)
LAST = E - (NG - 1) * GE
W = P // 3
NP = N + W
GT = NG // 2
RING = 8
EPS_MSG, EPS = 1e-7, 1e-5
TINY = 1e-37
RANGE = 60.0


class At:

    def __init__(self, base, off):
        self.base, self.off = base, off

    def __sub__(self, lag):
        return At(self.base, self.off - lag)

    def inside(self, n):
        return self.base is not None or 0 <= self.off < n

    def times(self, m, c=0):
        return self.off * m + c if self.base is None else self.base * m + (self.off * m + c)


def pipeline(e, n, unroll, peel, tail, body):
    end = peel + (n - peel - 1) // unroll * unroll
    for i in range(peel):
        body(At(None, i))
    with e.Fori(peel, end, unroll) as base:
        base = e.bass.s_assert_within(base, peel, end - unroll,
                                      skip_runtime_bounds_check_because="the loop counts by its step")
        for u in range(unroll):
            body(At(base, u))
    for i in range(end, n + tail):
        body(At(None, i))


def wait(e, sem, i, m=1, c=None):
    v = i.times(m, m if c is None else c)
    if not isinstance(v, int) or v > 0:
        e.wait_ge(sem, v)


def gnn_kernel(nc, a, out):
    with ExitStack() as ctx:
        def sb(name, shape, dt=F32):
            return ctx.enter_context(nc.sbuf_tensor(name, shape, dt))

        def sem(name):
            return ctx.enter_context(nc.semaphore(name))

        def dram(name, shape, dt=F32):
            return nc.dram_tensor(name, shape, dt, kind="Internal").ap()

        x_mid = dram("x_mid", [N, D])
        msg_table = dram("msg_table", [N, D])
        h_table = dram("h_table", [N, ROW])
        h_parts = dram("h_parts", [3, NP, ROW], BF16)
        e0_few = dram("e0_few", [NG, P, GE])
        dst_pad = dram("dst_pad", [NG, GE], I32)
        rel_rows = dram("rel_rows", [NG, J, P], BF16)

        xT_all = sb("xT", [P, 2 * NCH * D])
        xT = xT_all[:, 0:N]
        acc = sb("acc", [P, 2, NP])
        hid = acc
        x_rows = acc[0:TILE, :, :].rearrange("p k n -> p (k n)")[:, 0:2 * NCH * D].rearrange("p (t d) -> p t d", d=D)
        mid_rows = xT_all[0:TILE, :].rearrange("p (t d) -> p t d", d=D)
        nw1_pair = sb("nw1_pair", [P, P])
        ew1_pair = sb("ew1_pair", [P, P])
        ew2_pair = sb("ew2_pair", [P, P])
        ew0_pair = sb("ew0_pair", [P, P])
        few0_e = [sb(f"few0_e{k}", [P, P]) for k in range(2)]
        few0_h = sb("few0_h", [P, P])
        Z0 = sb("Z0", [P, NP])
        Z1, Z2 = acc[:, 0, :], acc[:, 1, :]
        ring = sb("ring", [P, RING, J, 320])
        msg = ring[:, :, :, 0:D]
        ex = ring[:, :, :, D:2 * D]
        onehot = sb("onehot", [P, RING, J, P])
        spare = sb("spare", [P, 4, GE])
        onehotT, relb = (spare[0:3 * W, 2 * k:2 * k + 2, :].rearrange("p b q -> p (b q)").bitcast(BF16)
                         .rearrange("p (b q) -> p b q", b=4) for k in range(2))
        window = sb("window", [3 * W, RING, ROW], BF16)
        work = sb("work", [P, 6, GE])
        src_idx = sb("src_idx", [P, NG, J], I32)
        idx_ring = sb("idx_ring", [P, RING, J], I32)
        rel = sb("rel", [P, NG, J])
        starts = sb("starts", [1, NG], I32)
        shifts = sb("shifts", [1, NG], I32)
        slot = ring[:, :, :, :].rearrange("p s j c -> p s (j c)")
        idx_i, idx2 = (slot[0:GT, s, 0:2 * GE].bitcast(I32).rearrange("g (k q) -> g k q", k=2) for s in (0, 1))
        relw = slot[0:GT, 2, 0:GE].bitcast(BF16).rearrange("g (k q) -> g k q", k=2)
        idx_f = work[0:GT, 0:4, :]
        ident = sb("ident", [P, P])
        iota_w = sb("iota_w", [P, W])
        iota_p = sb("iota_p", [P, 1])
        iota_t = sb("iota_t", [P, 4])
        ones = sb("ones", [1, P])
        stat = sb("stat", [P, 2, NCH, 6])
        mv = sb("mv", [P, 3, 2 * NCH])
        rstat = slot[0:TILE, 7, 0:2 * NCH * 6].rearrange("p (t s) -> p t s", s=6)
        sc = sb("sc", [P, 2 * NCH])
        sh = sb("sh", [P, 2 * NCH])
        cmax = sb("cmax", [P, NCH])
        small = sb("small", [P, 16])
        row = sb("row", [1, 2, NG])
        negc = sb("negc", [P, 1])
        flag = sb("flag", [1, 2], I32)
        W1 = sb("W1", [P, HID])
        W2 = sb("W2", [P, 2, D])
        b1, gam, bet = (sb(n, [P, 2]) for n in ("b1", "gam", "bet"))
        b2 = sb("b2", [P, 1])
        vecs = sb("vecs", [P, 4 * L])
        wraw = slot[:, 3:6, :].rearrange("p s q -> p (s q)")[:, 0:11 * P].rearrange("p (n c) -> p n c", n=11)
        lin = {n: sb(n, [P, P]) for n in ("nw0", "few0", "few1", "fnw0", "fnw1", "fnw2")}
        lin |= {n: sb(n, [P, HALF]) for n in ("nw1", "nw2", "ew0", "ew1", "ew2")}

        ps = [ctx.enter_context(nc.psum_tensor(f"ps{i}", [P, 512], F32)) for i in range(8)]


        def cols(i):
            return bass.ds(i.times(CH), CH) if not isinstance(i.times(CH), int) else slice(i.off * CH, (i.off + 1) * CH)

        def rows_of(t, i):
            v = t.rearrange("(c k p) d -> c p k d", p=TILE, k=2)
            return v[i.off, :, :, :] if i.base is None else v[bass.ds(i.times(1), 1), :, :, :].rearrange("o p k d -> (o p) k d")

        def pair(k, width=CH):
            return [work[:, k, b * 256:b * 256 + width] for b in range(2)]

        def rowring(k):
            return [work[0:TILE, k + b // 2, b % 2 * 256:b % 2 * 256 + 2 * D].rearrange("p (k d) -> p k d", k=2) for b in range(4)]

        def stores(e, S, names, n):
            for b, name in enumerate(names):
                e.wait_ge(S(name), 16 * len(range(b, n, len(names))))

        def begin(e, S):
            e.sem_inc(S("issued"), 1)

        phases = []
        TABLE = ["table0", "table1", "table2", "table3"]

        MATS = [("nw0", 0), ("nw1", 0), ("nw2", 0), ("ew0", 0), ("ew1", 0), ("ew2", 0),
                ("few0", 1), ("few1", 0), ("fnw0", 0), ("fnw1", 0), ("fnw2", 1)]

        def setup_sync(e, S):
            e.wait_ge(S("pads"), 2)
            for k, name in enumerate(("src", "dst")):
                for h, t in enumerate((idx_i, idx2)):
                    full = GT if h == 0 else NG - 1 - GT
                    v = a[name][h * GT * GE:(h * GT + full) * GE].rearrange("(g q) -> g q", q=GE)
                    e.dma_start(t[0:full, k, :], v).then_inc(S("indices"), 16)
                e.dma_start(idx2[GT - 1:GT, k, 0:LAST],
                            a[name][(NG - 1) * GE:E].rearrange("(g q) -> g q", g=1)).then_inc(S("indices"), 16)
            e.dma_start(starts[:, :], a["dst"][0:(NG - 1) * GE + 1:GE].rearrange("(g q) -> g q", g=1),
                        allow_slow_non_contiguous=True).then_inc(S("starts"), 16)
            e.wait_ge(S("indices"), 16 * 6)
            for h, t in enumerate((idx_i, idx2)):
                e.dma_start(dst_pad[h * GT:(h + 1) * GT, :], t[:, 1, :]).then_inc(S("pad_out"), 16)
            for l in range(L):
                for k, n in enumerate(("fnb", "feb", "g", "b")):
                    e.dma_start(vecs[:, 4 * l + k:4 * l + k + 1],
                                a[f"L1_gnn_{n}{l}"].rearrange("(k o) -> k o", o=1)).then_inc(S("vecs"), 16)
            for n, (name, swap) in enumerate(MATS):
                w = a["L1_gnn_" + name]
                r, c = w.shape
                halves = ((HALF, 0) if swap else (0, HALF)) if c > HALF else (0, 0)
                for k, c0 in enumerate(halves):
                    e.dma_start(wraw[0:r, n, k * HALF:(k + 1) * HALF], w[:, c0:c0 + HALF]).then_inc(S("weights"), 16)
            for h in range(2):
                e.wait_ge(S("relw"), h + 1)
                e.dma_start(rel_rows[h * GT:(h + 1) * GT, :, :].rearrange("g j p -> g (j p)"),
                            relw[:, h, :]).then_inc(S("rel_out"), 16)
            e.wait_ge(S("rel_out"), 32)
            e.wait_ge(S("pad_out"), 32)
            e.wait_ge(S("vecs"), 16 * 4 * L)
            e.wait_ge(S("starts"), 16)

        def setup_act(e, S):
            e.dma_start(x_rows, a["x"].rearrange("(t p) d -> p t d", p=TILE)).then_inc(S("x_rows"), 16)
            e.wait_ge(S("x_rows"), 16)

        def setup_pool(e, S):
            e.memset(ident[:, :], 1.0).then_inc(S("const"), 1)
            e.wait_ge(S("const"), 1)
            e.affine_select(out=ident[:, :], in_=ident[:, :], compare_op=ALU.is_equal, fill=0.0, base=0,
                            pattern=[[-1, P]], channel_multiplier=1).then_inc(S("const"), 1)
            e.iota(iota_w[:, :], pattern=[[1, W]], base=0, channel_multiplier=0,
                   allow_small_or_imprecise_dtypes=True).then_inc(S("const"), 1)
            e.iota(iota_t[:, 0:1], pattern=[[0, 1]], base=0, channel_multiplier=1,
                   allow_small_or_imprecise_dtypes=True).then_inc(S("const"), 1)
            e.memset(ones[:, :], 1.0).then_inc(S("const"), 1)
            e.memset(Z0[:, :], 0.0).then_inc(S("const"), 1)
            e.memset(ew0_pair[:, :], 0.0).then_inc(S("const"), 1)
            for t in (*few0_e, few0_h):
                e.memset(t[:, :], 0.0).then_inc(S("const"), 1)
            e.memset(xT_all[:, N:NP], 0.0).then_inc(S("zeros"), 1)
            e.memset(onehot[:, :, :, :], 0.0).then_inc(S("zeros"), 1)
            e.wait_ge(S("zeros"), 2)

        def setup_pe(e, S):
            e.wait_ge(S("const"), 10)
            e.wait_ge(S("weights"), 32 * len(MATS))
            for n, (name, _) in enumerate(MATS):
                r = a["L1_gnn_" + name].shape[0]
                if n >= 2:
                    e.wait_ge(S("turned_copy"), n - 1)
                e.transpose(ps[n % 2][:, 0:r], wraw[0:r, n, :], ident[0:r, 0:r]).then_inc(S("turned"), 1)
            e.wait_ge(S("idx_f"), 2)
            for n in range(4 * J):
                h, k, j = n // (2 * J), n // J % 2, n % J
                if n >= 2:
                    e.wait_ge(S("idx_copy"), n - 1)
                e.transpose(ps[2 + n % 2][:, 0:GT], idx_f[:, 2 * h + k, j:GE:J],
                            ident[0:GT, 0:GT]).then_inc(S("idx_turned"), 1)
            e.wait_ge(S("worst"), 1)
            e.transpose(ps[4][0:1, 0:GT], small[0:GT, 8:9], ident[0:GT, 0:GT]).then_inc(S("worst_row"), 1)

        def setup_dve(e, S):
            def then(ins):
                ins.then_inc(S("v"), 1)
                then.n += 1
                e.wait_ge(S("v"), then.n)
            then.n = 0
            e.memset(idx2[:, 0, :], 0).then_inc(S("pads"), 1)
            e.memset(idx2[:, 1, :], N).then_inc(S("pads"), 1)
            e.wait_ge(S("const"), 10)
            then(e.tensor_scalar(iota_t[:, 1:2], iota_t[:, 0:1], float(W), -float(W), ALU.is_ge, ALU.mult))
            then(e.tensor_scalar(iota_t[:, 2:3], iota_t[:, 0:1], 2.0 * W, -float(W), ALU.is_ge, ALU.mult))
            then(e.tensor_tensor(iota_t[:, 3:4], iota_t[:, 1:2], iota_t[:, 2:3], ALU.add))
            then(e.tensor_tensor(iota_p[:, :], iota_t[:, 0:1], iota_t[:, 3:4], ALU.add))
            e.wait_ge(S("indices"), 16 * 6)
            then(e.tensor_copy(idx_f[:, 0:2, :], idx_i))
            then(e.tensor_copy(idx_f[:, 2:4, :], idx2))
            for h in range(2):
                then(e.tensor_copy(small[0:GT, h:h + 1], idx_f[:, 2 * h + 1, 0:1]))
                e.tensor_scalar(idx_f[:, 2 * h + 1, :], idx_f[:, 2 * h + 1, :], small[0:GT, h:h + 1], None,
                                ALU.subtract).then_inc(S("idx_f"), 1)
                e.wait_ge(S("idx_f"), h + 1)
                e.tensor_copy(relw[:, h, :].rearrange("g (j p) -> g j p", j=J),
                              idx_f[:, 2 * h + 1, :].rearrange("g (p j) -> g j p", j=J)).then_inc(S("relw"), 1)
            for h in range(2):
                then(e.tensor_reduce(small[0:GT, 2 + h:3 + h], idx_f[:, 2 * h + 1, :], AX, ALU.max))
                then(e.tensor_reduce(small[0:GT, 4 + h:5 + h], idx_f[:, 2 * h + 1, :], AX, ALU.min))
                then(e.tensor_scalar(small[0:GT, 4 + h:5 + h], small[0:GT, 4 + h:5 + h], -float(W), None, ALU.mult))
            then(e.tensor_reduce(small[0:GT, 8:9], small[0:GT, 2:6], AX, ALU.max))
            e.sem_inc(S("worst"), 1)
            for n, (name, _) in enumerate(MATS):
                r = a["L1_gnn_" + name].shape[0]
                e.wait_ge(S("turned"), n + 1)
                e.tensor_copy(lin[name][:, 0:r], ps[n % 2][:, 0:r]).then_inc(S("turned_copy"), 1)
            then(e.tensor_copy(lin["nw0"][:, HALF:P], lin["nw0"][:, 0:HALF]))
            for name, pair in (("nw1", nw1_pair), ("ew1", ew1_pair), ("ew2", ew2_pair)):
                for h in (slice(0, HALF), slice(HALF, P)):
                    then(e.tensor_copy(pair[:, h], lin[name][:, :]))
            for h in (slice(0, HALF), slice(HALF, P)):
                then(e.tensor_copy(ew0_pair[h, h], lin["ew0"][h, :]))
            lo, hi = slice(0, HALF), slice(HALF, P)
            then(e.tensor_copy(few0_e[0][lo, :], lin["few0"][lo, :]))
            then(e.tensor_copy(few0_e[1][hi, :], lin["few0"][lo, :]))
            then(e.tensor_copy(few0_h[hi, :], lin["few0"][hi, :]))
            for n in range(4 * J):
                h, k, j = n // (2 * J), n // J % 2, n % J
                e.wait_ge(S("idx_turned"), n + 1)
                e.tensor_copy((rel if k else src_idx)[:, h * GT:(h + 1) * GT, j],
                              ps[2 + n % 2][:, 0:GT]).then_inc(S("idx_copy"), 1)
            e.wait_ge(S("worst_row"), 1)
            then(e.tensor_reduce(small[0:1, 9:10], ps[4][0:1, 0:GT], AX, ALU.max))
            then(e.tensor_scalar(small[0:1, 10:11], small[0:1, 9:10], float(W), None, ALU.is_ge))
            then(e.tensor_copy(flag[0:1, 1:2], small[0:1, 10:11]))
            e.wait_ge(S("starts"), 16)
            then(e.tensor_copy(row[:, 0, :], starts[:, :]))
            then(e.memset(row[:, 1, :], 0.0))
            then(e.tensor_tensor(row[:, 1, 1:NG], row[:, 0, 1:NG], row[:, 0, 0:NG - 1], ALU.subtract))
            then(e.tensor_scalar(row[:, 1, :], row[:, 1, :], float(W), 0.0, ALU.min, ALU.max))
            then(e.tensor_copy(shifts[:, :], row[:, 1, :]))
            e.wait_ge(S("vecs"), 16 * 4 * L)
            for l in range(L):
                g = vecs[:, 4 * l + 2:4 * l + 3]
                then(e.tensor_scalar(g, g, (1.0 + EPS) ** -0.5, None, ALU.mult))

        SETUP = "x_rows pad_out zeros pads indices starts vecs weights relw rel_out const turned turned_copy idx_f idx_copy idx_turned worst worst_row v".split()
        phases.append(("setup", SETUP, dict(sync=setup_sync, pool=setup_pool, act=setup_act, pe=setup_pe, dve=setup_dve)))

        def shift_pe(e, S):
            e.wait_ge(S("max_col"), 1)
            e.transpose(ps[2][0:1, 0:P], small[:, 11:12], ident[:, :]).then_inc(S("max_row"), 1)
            e.wait_ge(S("max_one"), 1)
            e.matmul(ps[3][:, 0:1], ones[:, :], small[0:1, 12:13], start=True, stop=True).then_inc(S("max_all"), 1)

        def shift_dve(e, S):
            e.tensor_reduce(small[:, 11:12], cmax[:, :], AX, ALU.max).then_inc(S("max_col"), 1)
            e.wait_ge(S("max_row"), 1)
            e.tensor_reduce(small[0:1, 12:13], ps[2][0:1, 0:P], AX, ALU.max).then_inc(S("max_one"), 1)
            e.wait_ge(S("max_all"), 1)
            e.tensor_scalar(negc[:, :], ps[3][:, 0:1], -1.0, None, ALU.mult).then_inc(S("shift"), 1)
            e.tensor_scalar(small[0:1, 13:14], small[0:1, 12:13], RANGE, small[0:1, 10:11], ALU.is_gt, ALU.max).then_inc(S("shift"), 1)
            e.wait_ge(S("shift"), 2)
            e.tensor_copy(flag[0:1, 0:1], small[0:1, 13:14]).then_inc(S("shift"), 1)

        SHIFT = "max_col max_row max_one max_all shift".split()

        def row_stats(e, S, rows, i, t=None):
            if i.base is None:
                q = i.off if t is None else 2 * i.off + t
                return e.bn_stats(rstat[:, q, :], rows[:, q, :])
            q = bass.ds(i.times(1) if t is None else i.times(2, t), 1)
            return e.bn_stats(rstat[:, q, :].rearrange("p o s -> p (o s)"), rows[:, q, :].rearrange("p o d -> p (o d)"))

        def row_scales(e, S):
            v = [0]

            def then(ins):
                v[0] += 1
                ins.then_inc(S("scale"), 1)
                e.wait_ge(S("scale"), v[0])
            m0, q0, m1, q1 = (rstat[:, :, k] for k in (1, 2, 4, 5))
            mean, var, diff = (mv[0:TILE, k, :] for k in range(3))
            then(e.tensor_tensor(mean, m0, m1, ALU.add))
            then(e.tensor_scalar(mean, mean, 0.5, None, ALU.mult))
            then(e.tensor_tensor(diff, m0, m1, ALU.subtract))
            then(e.tensor_scalar(diff, diff, 0.5, None, ALU.mult))
            then(e.tensor_tensor(diff, diff, diff, ALU.mult))
            then(e.tensor_tensor(var, q0, q1, ALU.add))
            then(e.tensor_scalar(var, var, 1.0 / D, EPS, ALU.mult, ALU.add))
            then(e.tensor_tensor(sc[0:TILE, :], var, diff, ALU.add))
            e.sem_inc(S("var"), 1)
            e.wait_ge(S("root"), 1)
            then(e.reciprocal(sc[0:TILE, :], sc[0:TILE, :]))
            then(e.tensor_tensor(sh[0:TILE, :], mean, sc[0:TILE, :], ALU.mult))
            then(e.tensor_scalar(sh[0:TILE, :], sh[0:TILE, :], -1.0, None, ALU.mult))
            e.sem_inc(S("norm"), 1)

        def row_roots(e, S):
            e.wait_ge(S("var"), 1)
            e.activation(sc[0:TILE, :], sc[0:TILE, :], ACT.Sqrt).then_inc(S("root"), 1)
            e.wait_ge(S("norm"), 1)

        def normalized(e, rows, i, to):
            for k in range(2):
                t = 2 * i.off + k
                if i.base is None:
                    src, s1, s2 = rows[:, t, :], sc[0:TILE, t:t + 1], sh[0:TILE, t:t + 1]
                else:
                    q = bass.ds(i.times(2, k), 1)
                    src = rows[:, q, :].rearrange("p o d -> p (o d)")
                    s1, s2 = sc[0:TILE, q], sh[0:TILE, q]
                ins = e.activation(to[:, k, :], src, ACT.Relu, bias=s2, scale=s1)
            return ins

        def norm_phase():
            hrow = rowring(0)

            def sync(e, S):
                def step(i):
                    wait(e, S("h"), i)
                    begin(e, S)
                    e.dma_start(rows_of(msg_table, i), hrow[i.off % 4]).then_inc(S(TABLE[i.off % 4]), 16)
                pipeline(e, NCH, 4, 4, 0, step)
                stores(e, S, TABLE, NCH)

            def dve(e, S):
                pipeline(e, 2 * NCH, 10, 10, 0, lambda i: row_stats(e, S, x_rows, i).then_inc(S("stats"), 1))
                e.wait_ge(S("stats"), 2 * NCH)
                row_scales(e, S)

                def copy(i):
                    if i.inside(NCH):
                        wait(e, S("turn"), i)
                        e.tensor_copy(xT[:, cols(i)], ps[4 + i.off % 4][:, 0:CH]).then_inc(S("xT"), 1)
                    if (i - 1).inside(NCH):
                        wait(e, S("xT"), i - 1)
                        k = i - 1
                        c = slice(k.off, k.off + 1) if k.base is None else bass.ds(k.times(1), 1)
                        e.tensor_reduce(cmax[:, c], xT[:, cols(k)], AX, ALU.max).then_inc(S("cmax"), 1)
                pipeline(e, NCH, 4, 4, 1, copy)
                e.wait_ge(S("cmax"), NCH)
                shift_dve(e, S)

            def act(e, S):
                row_roots(e, S)

                def step(i):
                    wait(e, S("turn"), i - 4)
                    wait(e, S(TABLE[i.off % 4]), i, 4, -4 * (i.off % 4))
                    normalized(e, x_rows, i, hrow[i.off % 4]).then_inc(S("h"), 1)
                pipeline(e, NCH, 4, 4, 0, step)

            def pe(e, S):
                def step(i):
                    wait(e, S("h"), i)
                    wait(e, S("xT"), i - 4)
                    for k in range(2):
                        ins = e.transpose(ps[4 + i.off % 4][:, k * TILE:(k + 1) * TILE], hrow[i.off % 4][:, k, :],
                                          ident[0:TILE, 0:TILE])
                    ins.then_inc(S("turn"), 1)
                pipeline(e, NCH, 4, 4, 0, step)
                shift_pe(e, S)

            names = "issued table0 table1 table2 table3 stats var root scale norm h turn xT cmax".split() + SHIFT
            return ("norm", names, dict(sync=sync, act=act, pe=pe, dve=dve))

        phases.append(norm_phase())

        def hidden_general(who, e, S):
            quot = [work[:, b, 0:CH] for b in range(2)]
            if who == "dve":
                def step(i):
                    b = quot[i.off % 2]
                    wait(e, S("W1"), i - 2)
                    e.reciprocal(b, acc[:, 0, cols(i)]).then_inc(S("quot"), 1)
                    wait(e, S("quot"), i, 3, 1)
                    e.tensor_tensor(b, b, acc[:, 1, cols(i)], ALU.mult).then_inc(S("quot"), 1)
                    wait(e, S("quot"), i, 3, 2)
                    e.tensor_tensor(b, b, xT[:, cols(i)], ALU.add).then_inc(S("quot"), 1)
                pipeline(e, NCH, 2, 2, 0, step)
            if who == "pe":
                def step(i):
                    wait(e, S("quot"), i, 3)
                    wait(e, S("hid"), i - 2)
                    for h in range(2):
                        ins = e.matmul(ps[i.off % 2][:, h * 256:h * 256 + CH], W1[:, h * P:(h + 1) * P], quot[i.off % 2],
                                       start=True, stop=True)
                    ins.then_inc(S("W1"), 1)
                pipeline(e, NCH, 2, 2, 0, step)
            if who == "act":
                hidden_columns(e, S)

        def hidden_columns(e, S):
            def step(i):
                wait(e, S("W1"), i)
                for h in range(2):
                    ins = e.activation(hid[:, h, cols(i)], ps[i.off % 2][:, h * 256:h * 256 + CH], ACT.Identity,
                                       bias=b1[:, h:h + 1])
                ins.then_inc(S("hid"), 1)
            pipeline(e, NCH, 2, 2, 0, step)

        drow = sb("drow", [1, GE], I32)
        dst_cols = sb("dst_cols", [P, 2 * J], I32)
        greatest = slot[:, 2:8, :].rearrange("p s q -> p (s q)")[:, 0:NP]

        def relay(sweeps):
            def part(who, e, S):
                before = 1
                if who == "dve":
                    e.sem_inc(S("baton"), 1)
                for turns in sweeps:
                    def lap(g):
                        for k, (owner, step) in enumerate(turns):
                            if owner == who:
                                e.wait_ge(S("baton"), g.times(len(turns), k + before))
                                begin(e, S)
                                step(e, S, g)
                                begin(e, S)
                                e.drain()
                                e.sem_inc(S("baton"), 1)
                    with e.Fori(0, NG - 1, 1) as base:
                        lap(At(base, 0))
                    lap(At(None, NG - 1))
                    before += len(turns) * NG
                e.wait_ge(S("baton"), before)
                e.drain()
            return part

        def either(column, general, parts):
            def of(who):
                def run(e, S):
                    needed = e.value_load(flag[0:1, column:column + 1], min_val=0, max_val=1)
                    with e.If(needed):
                        general(who, e, S)
                    with e.Else():
                        parts[who](e, S)
                return run
            return {who: of(who) for who in ("sync", "pool", "act", "pe", "dve")}

        def bias(l, k):
            return vecs[:, 4 * l + k:4 * l + k + 1]

        def one(g):
            return bass.ds(g.times(1), 1)

        def serial(e, per_edge):
            with e.Fori(0, P, 1) as p:
                for j in range(J):
                    d = e.value_load(drow[0:1, bass.ds(p * J + j, 1)], min_val=0, max_val=N)
                    per_edge(bass.ds(p + j * P, 1), bass.ds(d, 1))
                    e.drain()

        def all_gather(name, jobs):
            def step(e, S, g):
                for table, dst, idx in jobs:
                    for j in range(J):
                        e.indirect_dma_start(out=dst[:, j, :], out_offset=None, in_=table,
                                             in_offset=bass.IndirectOffsetOnAxis(ap=idx[:, j:j + 1], axis=0)
                                             ).then_inc(S("gather_all_" + name), 16)
                m = 16 * J * len(jobs)
                e.wait_ge(S("gather_all_" + name), g.times(m, m))
            return step

        def take_sources(e, S, g):
            e.activation(idx_ring[:, 0, :].rearrange("p (o j) -> p o j", o=1), src_idx[:, one(g), :], ACT.Copy)

        def take_destinations(name):
            def step(e, S, g):
                e.dma_start(drow[:, :], dst_pad[one(g), :]).then_inc(S(name), 16)
                e.wait_ge(S(name), g.times(16, 16))
            return step

        def turn_rows(bank, rows, width=P):
            def step(e, S, g):
                for j in range(J):
                    e.transpose(bank[0:width, j * P:(j + 1) * P], rows[:, j, :], ident[:, :])
            return step

        def few0_of(e, bank, t, e0T):
            to = bank[:, :].rearrange("p (h t a q) -> p t h a q", h=2, t=2, a=2)[:, t, :, :, :]
            return e.matmul(to, few0_e[t][:, :], e0T.rearrange("p (h a) q -> p h a q", a=2), start=True, stop=True)

        def edges_general(attr, term):
            m, ex_m, exps = work[:, 0, :], work[:, 1:3, :], work[:, 1, :]
            ea, eaT = (work[:, k, 0:2 * P] for k in (3, 4))
            e0T = work[0:HALF, 5, :]
            er = ring[:, 1, :, 2 * D:2 * D + HALF]
            term_out = spare[:, 0, :]

            def maxima(e, S, g):
                e.tensor_scalar(m, ps[0][:, :], EPS_MSG, None, ALU.add)
                e.drain()
                serial(e, lambda c, d: e.tensor_tensor(greatest[:, d], greatest[:, d], m[:, c], ALU.max))

            def minus(e, S, g):
                e.tensor_scalar(m, ps[0][:, :], EPS_MSG, None, ALU.add)
                e.drain()
                serial(e, lambda c, d: e.tensor_tensor(exps[:, c], m[:, c], greatest[:, d], ALU.subtract))

            def exp(e, S, g):
                e.activation(exps, exps, ACT.Exp)

            def sums(e, S, g):
                e.tensor_tensor(work[:, 2, :], exps, m, ALU.mult)
                e.drain()
                serial(e, lambda c, d: e.tensor_tensor(acc[:, :, d], acc[:, :, d], ex_m[:, :, c], ALU.add))

            def load_attr(e, S, g):
                v = ea.rearrange("p (j c) -> p j c", j=J)
                if g.base is None:
                    full = LAST // J
                    src = a["edge_attr_64"][(NG - 1) * GE:(NG - 1) * GE + full * J, :]
                    e.dma_start(v[0:full, :, :], src.rearrange("(p j) c -> p j c", j=J)).then_inc(S("all_ea"), 16)
                    e.dma_start(v[full:full + 1, 0:LAST - full * J, :],
                                a["edge_attr_64"][E - (LAST - full * J):E, :].rearrange("(o j) c -> o j c", o=1)).then_inc(S("all_ea"), 16)
                else:
                    e.dma_start(v, a["edge_attr_64"][bass.ds(g.times(GE), GE), :].rearrange("(p j) c -> p j c", j=J)).then_inc(S("all_ea"), 16)
                e.wait_ge(S("all_ea"), g.times(16, 16) if g.base is not None else 16 * (NG + 1))

            def turn_attr(e, S, g):
                for h in range(J // 2):
                    e.transpose(ps[2][:, h * P:(h + 1) * P], ea[:, h * P:(h + 1) * P], ident[:, :])

            def copy_attr(e, S, g):
                e.activation(eaT, ps[2][:, 0:2 * P], ACT.Copy)

            def first_layer(e, S, g):
                for h in range(J // 2):
                    e.matmul(ps[4][:, h * P:(h + 1) * P], eaT[:, h * P:(h + 1) * P], ew0_pair[:, :], start=True, stop=True)

            def relu_e0(e, S, g):
                e.tensor_scalar(er, ps[4][:, 0:J * HALF].rearrange("p (j c) -> p j c", j=J), 0.0, None, ALU.max)

            def first_layer_T(e, S, g):
                e.matmul(ps[4][:, 0:2 * P], ew0_pair[:, :], eaT, start=True, stop=True)

            def relu_e0T(e, S, g):
                e.tensor_scalar(er, ps[4][:, 0:2 * P].rearrange("p (j c) -> p j c", j=J), 0.0, None, ALU.max)

            def few_e0(e, S, g):
                for t in range(2):
                    few0_of(e, ps[5], t, er)

            def copy_term(e, S, g):
                e.activation(term_out, ps[5][:, :], ACT.Copy)

            def store_term(e, S, g):
                e.dma_start(e0_few[one(g), :, :].rearrange("o p q -> (o p) q"), term_out).then_inc(S("all_term"), 16)
                e.wait_ge(S("all_term"), g.times(16, 16))

            def sum_e0(e, S, g):
                e.tensor_copy(e0T, ps[5][0:HALF, :])
                e.drain()
                serial(e, lambda c, d: e.tensor_tensor(Z0[0:HALF, d], Z0[0:HALF, d], e0T[:, c], ALU.add))

            def fetch(k):
                return [("act", take_sources), ("sync", take_destinations(f"all_dst{k}")),
                        ("pool", all_gather(f"{layer}_{k}", [(msg_table, msg[:, 0, :, :], idx_ring[:, 0, :])])),
                        ("pe", turn_rows(ps[0], msg[:, 0, :, :]))]
            sweeps = [fetch(0) + [("dve", maxima)],
                      fetch(1) + [("dve", minus), ("act", exp), ("dve", sums)]]
            turned = [("sync", load_attr), ("pe", turn_attr), ("act", copy_attr)]
            if attr:
                sweeps.append(turned + [("pe", first_layer), ("dve", relu_e0), ("sync", take_destinations("all_dst2")),
                                        ("pe", turn_rows(ps[5], er, HALF)), ("dve", sum_e0)])
            if term:
                sweeps.append(turned + [("pe", first_layer_T), ("dve", relu_e0T), ("pe", few_e0), ("act", copy_term),
                                        ("sync", store_term)])
            passes = relay(sweeps)

            def part(who, e, S):
                if who == "dve":
                    e.memset(greatest, 0.0)
                    e.memset(acc[:, 0, :], TINY)
                    e.memset(acc[:, 1, :], 0.0)
                    e.drain()
                passes(who, e, S)
                if who in ("pe", "act"):
                    e.wait_ge(S("params"), 16 * 6)
                hidden_general(who, e, S)
            return part

        def edge_layers_general():
            X, A, T = work[:, 0, :], work[:, 1, :], work[:, 2, :]
            own, other = ring[:, 0, :, :], ring[:, 1, :, 0:ROW]
            dst_f = small[:, 0:J]

            def load_dst(e, S, g):
                e.dma_start(dst_cols[:, 0:J].rearrange("p (o j) -> p o j", o=1),
                            dst_pad[one(g), :].rearrange("o (p j) -> p o j", j=J)).then_inc(S("all_cols"), 16)
                e.wait_ge(S("all_cols"), g.times(16, 16))

            def clamp_dst(e, S, g):
                e.tensor_copy(dst_f, dst_cols[:, 0:J])
                e.drain()
                e.tensor_scalar(dst_f, dst_f, float(N - 1), None, ALU.min)
                e.drain()
                e.tensor_copy(dst_cols[:, J:2 * J], dst_f)

            def load_term(e, S, g):
                e.dma_start(X, e0_few[one(g), :, :].rearrange("o p q -> (o p) q")).then_inc(S("all_term"), 16)
                e.wait_ge(S("all_term"), g.times(16, 16))

            def both_ends(e, S, g):
                e.tensor_tensor(own[:, :, 0:ROW], own[:, :, 0:ROW], other, ALU.add)

            def add_term(e, S, g):
                e.tensor_tensor(X, X, ps[0][:, :], ALU.add)

            def relu_term(e, S, g):
                e.activation(A, X, ACT.Relu, bias=bias(0, 1))

            def copy(bank, dst):
                return lambda e, S, g: e.tensor_copy(dst, bank[:, :])

            def few(bank, name):
                return lambda e, S, g: e.matmul(bank[:, :], lin[name][:, :], X, start=True, stop=True)

            def relu(bank, l):
                return lambda e, S, g: e.activation(A, bank[:, :], ACT.Relu, bias=bias(l, 1))

            def ew(bank, pair):
                def step(e, S, g):
                    for j in range(J):
                        e.matmul(bank[:, j * P:(j + 1) * P], A[:, j * P:(j + 1) * P], pair[:, :], start=True, stop=True)
                return step

            def by_edge(bank, c0):
                return lambda e, S, g: e.activation(own[:, :, c0:c0 + HALF], bank[:, :].rearrange("p (j c) -> p j c", j=J)[:, :, 0:HALF], ACT.Relu)

            def sums(e, S, g):
                e.tensor_copy(T, ps[6][:, :])
                e.drain()
                lo, hi = slice(0, HALF), slice(HALF, P)

                def add(c, d):
                    e.tensor_tensor(Z1[lo, d], Z1[lo, d], T[lo, c], ALU.add)
                    e.tensor_tensor(Z2[hi, d], Z2[hi, d], T[hi, c], ALU.add)
                serial(e, add)

            return relay([[
                ("act", take_sources), ("sync", take_destinations("all_dst0")), ("sync", load_dst), ("dve", clamp_dst),
                ("pool", all_gather("h", [(h_table, own[:, :, 0:ROW], idx_ring[:, 0, :]),
                                          (h_table, other, dst_cols[:, J:2 * J])])),
                ("sync", load_term), ("dve", both_ends),
                ("pe", turn_rows(ps[0], own[:, :, 0:D])), ("dve", add_term), ("act", relu_term),
                ("pe", ew(ps[2], ew1_pair)), ("act", by_edge(ps[2], ROW)),
                ("pe", turn_rows(ps[3], own[:, :, D:2 * D])), ("dve", copy(ps[3], X)), ("pe", few(ps[4], "few1")), ("act", relu(ps[4], 1)),
                ("pe", ew(ps[5], ew2_pair)), ("act", by_edge(ps[5], ROW + HALF)),
                ("pe", turn_rows(ps[6], own[:, :, ROW:ROW + D])), ("dve", sums)]])

        ALL = "baton all_dst0 all_dst1 all_dst2 all_ea all_term all_cols".split()

        def gathers(e, S, i, table, dst, tag):
            s = i.off % RING
            wait(e, S("idx"), i)
            begin(e, S)
            for j in range(J):
                e.indirect_dma_start(out=dst[:, s, j, :], out_offset=None, in_=table,
                                     in_offset=bass.IndirectOffsetOnAxis(ap=idx_ring[:, s, j:j + 1], axis=0)
                                     ).then_inc(S(f"gather{tag}_{s}"), 16)

        def gathered(e, S, i, tag):
            wait(e, S(f"gather{tag}_{i.off % RING}"), i, 8, 64 - 8 * (i.off % RING))

        def first_indices(e, S):
            for g in range(RING):
                e.activation(idx_ring[:, g, :], src_idx[:, g, :], ACT.Copy).then_inc(S("idx"), 1)

        def next_indices(e, S, i):
            if i.base is not None or i.off + RING < NG:
                e.activation(idx_ring[:, i.off % RING, :].rearrange("p (o j) -> p o j", o=1),
                             src_idx[:, bass.ds(i.times(1, RING), 1), :], ACT.Copy).then_inc(S("idx"), 1)

        def make_onehot(e, i, onehot=onehot):
            g = bass.ds(i.times(1), 1)
            to = rel[:, g, :].rearrange("p o j -> p (o j)").rearrange("p (j o) -> p j o", o=1).broadcast_to([P, J, W])
            at = iota_w[:, :].rearrange("p (o w) -> p o w", o=1).broadcast_to([P, J, W])
            return e.tensor_tensor(onehot[:, i.off % RING, :, 0:W], to, at, ALU.is_equal)

        def window_start(e, i):
            return e.value_load(starts[0:1, bass.ds(i.times(1), 1)], min_val=0, max_val=N - 1)

        def edges_phase(layer):
            attr, term = layer == 0, layer == 1
            both = attr or term
            ea = [work[:, s, 0:J * DE].rearrange("p (j c) -> p j c", j=J) for s in range(4)]
            eaT = [work[:, 4 + s, 0:2 * P] for s in range(2)]
            er = [ring[:, s, :, 2 * D:2 * D + HALF] for s in range(RING)]
            e0T = [ring[:, s, :, 2 * D:2 * D + HALF] for s in range(RING)]
            term_out = [spare[:, b, :] for b in range(4)]
            sums = [work[:, s, 256:256 + 4 * W].rearrange("p (k w) -> p k w", k=2) for s in range(4)]
            aggr = [work[:, s, 256 + 4 * W:256 + 5 * W] for s in range(4)]
            node = [work[:, 4 + s, 256:256 + P] for s in range(2)]

            def loads(e, S):
                for t, n in ((b1, "b1"), (gam, "gamma"), (bet, "beta")):
                    e.dma_start(t[:, :], a["L0_gnn_" + n][layer, :].rearrange("(h k) -> k h", k=P),
                                allow_slow_non_contiguous=True).then_inc(S("params"), 16)
                e.dma_start(b2[:, :], a["L0_gnn_b2"][layer, :].rearrange("(k o) -> k o", o=1)).then_inc(S("params"), 16)
                e.dma_start(W1[:, :], a["L0_gnn_W1"][layer, :, :]).then_inc(S("params"), 16)
                e.dma_start(W2[:, :, :], a["L0_gnn_W2"][layer, :, :].rearrange("(h k) m -> k h m", k=P)).then_inc(S("params"), 16)

            def sync(e, S):
                if both:
                    def step(i):
                        if i.inside(NG):
                            wait(e, S("eaT"), i - 4)
                            begin(e, S)
                            s = i.off % 4
                            if i.base is None and i.off == NG - 1:
                                full = LAST // J
                                src = a["edge_attr_64"][(NG - 1) * GE:(NG - 1) * GE + full * J, :]
                                e.dma_start(ea[s][0:full, :, :], src.rearrange("(p j) c -> p j c", j=J)).then_inc(S(f"ea{s}"), 16)
                                e.dma_start(ea[s][full:full + 1, 0:LAST - full * J, :],
                                            a["edge_attr_64"][E - (LAST - full * J):E, :].rearrange("(o j) c -> o j c", o=1)).then_inc(S(f"ea{s}"), 16)
                            else:
                                src = a["edge_attr_64"][bass.ds(i.times(GE), GE), :]
                                e.dma_start(ea[s], src.rearrange("(p j) c -> p j c", j=J)).then_inc(S(f"ea{s}"), 16)
                        if term and (i - 4).inside(NG):
                            k = i - 4
                            wait(e, S("term"), k)
                            begin(e, S)
                            dst = e0_few[bass.ds(k.times(1), 1), :, :].rearrange("o p q -> (o p) q")
                            e.dma_start(dst, term_out[k.off % 4]).then_inc(S(f"term_out{k.off % 4}"), 16)
                    pipeline(e, NG, RING, RING, 4, step)
                    if term:
                        for s in range(4):
                            e.wait_ge(S(f"term_out{s}"), 16 * (NG // 4))

            def pool(e, S):
                def step(i):
                    wait(e, S("sums"), i - RING)
                    gathers(e, S, i, msg_table, msg, layer)
                pipeline(e, NG, RING, RING, 0, step)

            def act(e, S):
                first_indices(e, S)
                e.wait_ge(S("params"), 16 * 6)
                hidden_columns(e, S)
                e.wait_ge(S("hid"), NCH)

                def step(i):
                    if (i - 4).inside(NG):
                        k = i - 4
                        w = window_start(e, k)
                        wait(e, S("Wnode"), k)
                        wait(e, S("hid_w"), k - 1)
                        for h in range(2):
                            ins = e.activation(hid[:, h, bass.ds(w, W)], ps[2 + k.off % 2][:, 256 + h * P:256 + h * P + W],
                                               ACT.Identity, bias=b1[:, h:h + 1])
                        ins.then_inc(S("hid_w"), 1)
                    if i.inside(NG):
                        gathered(e, S, i, layer)
                        e.activation(ex[:, i.off % RING, :, :], msg[:, i.off % RING, :, :], ACT.Exp,
                                     bias=negc[:, :]).then_inc(S("exp"), 1)
                        next_indices(e, S, i)
                    if term and (i - 3).inside(NG):
                        k = i - 3
                        wait(e, S("few_e0"), k)
                        wait(e, S(f"term_out{k.off % 4}"), k, 4, -4 * (k.off % 4))
                        e.activation(term_out[k.off % 4], ps[6 + k.off % 2][:, :], ACT.Copy).then_inc(S("term"), 1)
                    if both and (i - 1).inside(NG):
                        k = i - 1
                        wait(e, S("ea_turned"), k)
                        wait(e, S("e0"), k - 2)
                        e.activation(eaT[k.off % 2], ps[2 + k.off % 2][:, 0:2 * P], ACT.Copy).then_inc(S("eaT"), 1)
                pipeline(e, NG, RING, 2 * RING if term else RING, 4, step)

            def pe(e, S):
                def without_edges(i):
                    wait(e, S("hid"), i - 2)
                    for h in range(2):
                        ins = e.matmul(ps[i.off % 2][:, h * 256:h * 256 + CH], W1[:, h * P:(h + 1) * P], xT[:, cols(i)],
                                       start=True, stop=True)
                    ins.then_inc(S("W1"), 1)
                e.wait_ge(S("params"), 16 * 6)
                pipeline(e, NCH, 2, 2, 0, without_edges)
                e.wait_ge(S("hid"), NCH)

                def step(i):
                    if i.inside(NG):
                        s, bank = i.off % RING, ps[i.off % 2]
                        if both:
                            last = i.base is None and i.off == NG - 1
                            wait(e, S(f"ea{i.off % 4}"), i, 4, 16 - 4 * (i.off % 4) + 16 * last)
                            wait(e, S("eaT"), i - 2)
                            wait(e, S("hid_w"), i - 4)
                            for h in range(J // 2):
                                pair = ea[i.off % 4][:, 2 * h:2 * h + 2, :].rearrange("p j c -> p (j c)")
                                ins = e.transpose(ps[2 + i.off % 2][:, h * P:(h + 1) * P], pair, ident[:, :])
                            ins.then_inc(S("ea_turned"), 1)
                    if attr and (i - 1).inside(NG):
                        k = i - 1
                        wait(e, S("eaT"), k)
                        wait(e, S("er"), k - 2)
                        for h in range(J // 2):
                            ins = e.matmul(ps[4 + k.off % 2][:, h * P:(h + 1) * P], eaT[k.off % 2][:, h * P:(h + 1) * P],
                                           ew0_pair[:, :], start=True, stop=True)
                        ins.then_inc(S("e0"), 1)
                    if term and (i - 1).inside(NG):
                        k = i - 1
                        wait(e, S("eaT"), k)
                        wait(e, S("e0T"), k - 2)
                        e.matmul(ps[4 + k.off % 2][:, 0:2 * P], ew0_pair[:, :], eaT[k.off % 2],
                                 start=True, stop=True).then_inc(S("e0"), 1)
                    if term and (i - 2).inside(NG):
                        k = i - 2
                        wait(e, S("e0T"), k)
                        wait(e, S("term"), k - 2)
                        for t in range(2):
                            ins = few0_of(e, ps[6 + k.off % 2], t, e0T[k.off % RING])
                        ins.then_inc(S("few_e0"), 1)
                    if (i - 3).inside(NG):
                        k = i - 3
                        wait(e, S("node"), k)
                        wait(e, S("hid_w"), k - 2)
                        for h in range(2):
                            ins = e.matmul(ps[2 + k.off % 2][:, 256 + h * P:256 + (h + 1) * P], W1[:, h * P:(h + 1) * P],
                                           node[k.off % 2], start=True, stop=True)
                        ins.then_inc(S("Wnode"), 1)
                    if attr and (i - 2).inside(NG):
                        k = i - 2
                        wait(e, S("er"), k)
                        wait(e, S("agg0"), k - 2)
                        for j in range(J):
                            ins = e.matmul(ps[6 + k.off % 2][0:HALF, 0:P], er[k.off % RING][:, j, :],
                                           onehot[:, k.off % RING, j, :], start=(j == 0), stop=(j == J - 1))
                        ins.then_inc(S("e0_sums"), 1)
                    if i.inside(NG):
                        wait(e, S("mexp"), i)
                        wait(e, S("acc"), i - 2)
                        for k, rows in enumerate((ex, msg)):
                            for j in range(J):
                                ins = e.matmul(bank[:, k * P:(k + 1) * P], rows[:, s, j, :], onehot[:, s, j, :],
                                               start=(j == 0), stop=(j == J - 1))
                        ins.then_inc(S("sums"), 1)
                pipeline(e, NG, RING, RING, 3, step)

            def dve(e, S):
                for t in sums:
                    e.memset(t[:, 0, :], TINY).then_inc(S("zero"), 1)
                    e.memset(t[:, 1, :], 0.0).then_inc(S("zero"), 1)
                for t in node:
                    e.memset(t, 0.0).then_inc(S("zero"), 1)
                e.wait_ge(S("zero"), 10)

                def step(i):
                    if i.inside(NG):
                        s = i.off % RING
                        wait(e, S("sums"), i - RING)
                        if attr:
                            wait(e, S("e0_sums"), i - RING)
                        make_onehot(e, i).then_inc(S("onehot"), 1)
                    if (i - 2).inside(NG):
                        k = i - 2
                        wait(e, S("acc"), k)
                        e.reciprocal(aggr[k.off % 4], sums[k.off % 4][:, 0, 0:W]).then_inc(S("quot"), 1)
                    if i.inside(NG):
                        wait(e, S("exp"), i)
                        e.scalar_tensor_tensor(out=msg[:, s, :, :], in0=msg[:, s, :, :], scalar=EPS_MSG,
                                               in1=ex[:, s, :, :], op0=ALU.add, op1=ALU.mult).then_inc(S("mexp"), 1)
                    if (i - 2).inside(NG):
                        t = aggr[k.off % 4]
                        wait(e, S("quot"), k, 2, 1)
                        e.tensor_tensor(t, t, sums[k.off % 4][:, 1, 0:W], ALU.mult).then_inc(S("quot"), 1)
                    if attr and (i - 1).inside(NG):
                        k = i - 1
                        wait(e, S("e0"), k)
                        s = k.off % RING
                        e.tensor_scalar(er[s], ps[4 + k.off % 2][:, 0:J * HALF].rearrange("p (j c) -> p j c", j=J), 0.0, None,
                                        ALU.max).then_inc(S("er"), 1)
                    if term and (i - 1).inside(NG):
                        k = i - 1
                        wait(e, S("e0"), k)
                        wait(e, S("few_e0"), k - RING)
                        e.tensor_scalar(e0T[k.off % RING], ps[4 + k.off % 2][:, 0:2 * P].rearrange("p (j c) -> p j c", j=J), 0.0,
                                        None, ALU.max).then_inc(S("e0T"), 1)
                    if (i - 1).inside(NG):
                        k = i - 1
                        by = e.value_load(shifts[0:1, bass.ds(k.times(1), 1)], min_val=0, max_val=W)
                        wait(e, S("sums"), k)
                        wait(e, S("acc"), k - 1)
                        new = ps[k.off % 2][:, 0:2 * P].rearrange("p (k w) -> p k w", k=2)[:, :, 0:W]
                        e.tensor_tensor(sums[k.off % 4][:, :, 0:W], sums[(k.off - 1) % 4][:, :, bass.ds(by, W)], new,
                                        ALU.add).then_inc(S("acc"), 1)
                    if (i - 2).inside(NG):
                        k = i - 2
                        w = window_start(e, k)
                        wait(e, S("quot"), k, 2, 2)
                        wait(e, S("Wnode"), k - 2)
                        e.tensor_tensor(node[k.off % 2][:, 0:W], aggr[k.off % 4], xT_all[:, bass.ds(w, W)],
                                        ALU.add).then_inc(S("node"), 1)
                    if attr and (i - 3).inside(NG):
                        k = i - 3
                        w = window_start(e, k)
                        wait(e, S("e0_sums"), k)
                        wait(e, S("agg0"), k - 1)
                        place = Z0[0:HALF, bass.ds(w, W)]
                        e.tensor_tensor(place, place, ps[6 + k.off % 2][0:HALF, 0:W], ALU.add).then_inc(S("agg0"), 1)
                pipeline(e, NG, RING, 2 * RING, 3 if attr else 2, step)

            names = ["params", "W1", "hid", "quot", "node", "Wnode", "hid_w", "issued", "eaT", "er", "exp", "ea_turned", "e0", "agg0", "e0_sums", "mexp", "acc", "sums", "zero",
                     "onehot", "idx"] + ["e0T", "few_e0", "term"] + [f"{n}{s}" for n in ("ea", "term_out") for s in range(4)]
            parts = either(0, edges_general(attr, term), dict(sync=sync, pool=pool, act=act, pe=pe, dve=dve))
            edges_sync = parts["sync"]

            def load_and_sync(e, S):
                loads(e, S)
                edges_sync(e, S)
                e.wait_ge(S("params"), 16 * 6)
            parts["sync"] = load_and_sync
            return ("edges", names + ALL, parts)


        def nodes_phase(last):
            hr = [work[:, b, 0:2 * CH].rearrange("p (h n) -> p h n", h=2) for b in range(4)]
            xc = [work[:, 4 + b // 2, b % 2 * 256:b % 2 * 256 + CH] for b in range(4)]
            hrow = [ring[0:TILE, b, 0, 0:2 * D].rearrange("p (k d) -> p k d", k=2) for b in range(4)]

            def pool(e, S):
                if last:
                    return

                def step(i):
                    wait(e, S("x_new"), i)
                    begin(e, S)
                    e.tensor_copy(xT[:, cols(i)], xc[i.off % 4]).then_inc(S("x_kept"), 1)
                pipeline(e, NCH, 4, 4, 0, step)

            def dve(e, S):
                def stats(k):
                    for h in range(2):
                        if k.base is None:
                            st = stat[:, h, k.off, :]
                        else:
                            st = stat[:, h, bass.ds(k.times(1), 1), :].rearrange("p o s -> p (o s)")
                        e.bn_stats(st, hid[:, h, cols(k)]).then_inc(S("stats"), 1)
                pipeline(e, NCH, 5, 5, 0, stats)
                e.wait_ge(S("stats"), 2 * NCH)
                v = [0]

                def then(ins):
                    v[0] += 1
                    ins.then_inc(S("scale"), 1)
                    e.wait_ge(S("scale"), v[0])
                for h in range(2):
                    then(e.bn_aggr(mv[:, h, 0:2], stat[:, h, :, :].rearrange("p c s -> p (c s)")))
                mean, var = (mv[:, 0:2, k] for k in range(2))
                then(e.tensor_scalar(sc[:, 0:2], var, EPS, None, ALU.add))
                e.sem_inc(S("var"), 1)
                e.wait_ge(S("root"), 1)
                then(e.reciprocal(sc[:, 0:2], sc[:, 0:2]))
                then(e.tensor_tensor(sc[:, 0:2], sc[:, 0:2], gam[:, :], ALU.mult))
                then(e.tensor_tensor(sh[:, 0:2], mean, sc[:, 0:2], ALU.mult))
                then(e.tensor_tensor(sh[:, 0:2], bet[:, :], sh[:, 0:2], ALU.subtract))
                e.sem_inc(S("norm"), 1)

                def out_rows(i):
                    if i.inside(NCH):
                        b = xc[i.off % 4]
                        wait(e, S("W2"), i)
                        wait(e, S("turn"), i - 4)
                        if not last:
                            wait(e, S("x_kept"), i - 4)
                            wait(e, S("cmax"), i - 4)
                        e.tensor_scalar(b, ps[i.off % 4][:, 0:CH], b2[:, :], 0.0, ALU.add, ALU.max).then_inc(S("x_new"), 1)
                    if not last and (i - 2).inside(NCH):
                        k = i - 2
                        wait(e, S("turn"), k)
                        wait(e, S(TABLE[k.off % 4]), k, 4, -4 * (k.off % 4))
                        e.tensor_copy(hrow[k.off % 4], ps[4 + k.off % 4][0:TILE, 0:2 * D].rearrange("p (k d) -> p k d", k=2)
                                      ).then_inc(S("rows"), 1)
                    if last and (i - 2).inside(NCH):
                        k = i - 2
                        at = slice(2 * k.off, 2 * k.off + 2) if k.base is None else bass.ds(k.times(2), 2)
                        wait(e, S("turn"), k)
                        e.tensor_tensor(mid_rows[:, at, :], mid_rows[:, at, :],
                                        ps[4 + k.off % 4][0:TILE, 0:2 * D].rearrange("p (k d) -> p k d", k=2), ALU.add).then_inc(S("rows"), 1)
                    if last and (i - 3).inside(NCH):
                        k = i - 3
                        wait(e, S("rows"), k)
                        for t in range(2):
                            row_stats(e, S, mid_rows, k, t).then_inc(S("row_stats"), 1)
                    if not last and (i - 1).inside(NCH):
                        k = i - 1
                        wait(e, S("x_new"), k)
                        c = slice(k.off, k.off + 1) if k.base is None else bass.ds(k.times(1), 1)
                        e.tensor_reduce(cmax[:, c], xc[k.off % 4], AX, ALU.max).then_inc(S("cmax"), 1)
                if last:
                    e.wait_ge(S("x_in"), 16)
                pipeline(e, NCH, 4, 8, 3 if last else 2, out_rows)
                if not last:
                    e.wait_ge(S("cmax"), NCH)
                    shift_dve(e, S)

            def act(e, S):
                e.wait_ge(S("var"), 1)
                e.activation(sc[:, 0:2], sc[:, 0:2], ACT.Sqrt).then_inc(S("root"), 1)
                e.wait_ge(S("norm"), 1)

                def out_rows(i):
                    if i.inside(NCH):
                        wait(e, S("W2"), i - 4)
                        for h in range(2):
                            ins = e.activation(hr[i.off % 4][:, h, :], hid[:, h, cols(i)], ACT.Relu,
                                               bias=sh[:, h:h + 1], scale=sc[:, h:h + 1])
                        ins.then_inc(S("hr"), 1)
                pipeline(e, NCH, 4, 4, 0, out_rows)

            def pe(e, S):
                def out_rows(i):
                    if i.inside(NCH):
                        wait(e, S("hr"), i)
                        wait(e, S("x_new"), i - 4)
                        for h in range(2):
                            ins = e.matmul(ps[i.off % 4][:, 0:CH], W2[:, h, :], hr[i.off % 4][:, h, :],
                                           start=(h == 0), stop=(h == 1))
                        ins.then_inc(S("W2"), 1)
                    if (i - 1).inside(NCH):
                        k = i - 1
                        wait(e, S("x_new"), k)
                        wait(e, S("rows"), k - 4)
                        for t in range(2):
                            ins = e.transpose(ps[4 + k.off % 4][0:TILE, t * D:(t + 1) * D],
                                              xc[k.off % 4][:, t * TILE:(t + 1) * TILE], ident[:, :])
                        ins.then_inc(S("turn"), 1)
                pipeline(e, NCH, 4, 8, 1, out_rows)
                if not last:
                    shift_pe(e, S)

            def sync(e, S):
                if last:
                    e.dma_start(mid_rows, a["x"].rearrange("(t p) d -> p t d", p=TILE)).then_inc(S("x_in"), 16)
                    e.wait_ge(S("x_in"), 16)
                    return

                def step(i):
                    wait(e, S("rows"), i)
                    begin(e, S)
                    e.dma_start(rows_of(msg_table, i), hrow[i.off % 4]).then_inc(S(TABLE[i.off % 4]), 16)
                pipeline(e, NCH, 4, 4, 0, step)
                stores(e, S, TABLE, NCH)

            names = "issued x_in row_stats x_new x_kept stats scale var root norm W2 turn cmax hr rows".split() + TABLE + SHIFT
            return ("nodes", names, dict(sync=sync, pool=pool, act=act, pe=pe, dve=dve))

        for layer in range(L):
            phases.append(edges_phase(layer))
            phases.append(nodes_phase(layer == L - 1))

        def hidden_phase():
            nrow = [ring[0:TILE, 4 + b, 2, 0:2 * D].rearrange("p (k d) -> p k d", k=2) for b in range(4)]
            xc = [work[:, 0, b * 256:b * 256 + CH] for b in range(2)]
            x1 = [work[:, 1, b * 256:b * 256 + CH] for b in range(2)]
            few_c = [work[:, 2 + b // 2, b % 2 * 256:b % 2 * 256 + CH] for b in range(4)]
            h1_c = [work[0:HALF, 4 + b // 2, b % 2 * 256:b % 2 * 256 + CH] for b in range(4)]
            part = [[ring[0:TILE, b, k, 0:ROW].bitcast(BF16).rearrange("p (k d) -> p k d", k=2) for k in range(3)]
                    for b in range(4)]
            rest = [spare[0:TILE, b, 0:2 * ROW].rearrange("p (k d) -> p k d", k=2) for b in range(2)]
            hrow = [ring[0:TILE, 4 + b, 0:2, 0:ROW] for b in range(4)]
            zero = spare[0:W, 2, 0:3 * ROW // 2].bitcast(BF16)

            def pe(e, S):
                def step(i):
                    if i.inside(NCH):
                        wait(e, S("n"), i)
                        wait(e, S("xc"), i - 1)
                        for t in range(2):
                            ins = e.transpose(ps[3][:, t * TILE:(t + 1) * TILE], nrow[i.off % 4][:, t, :], ident[0:TILE, 0:TILE])
                        ins.then_inc(S("n_turn"), 1)
                    if (i - 1).inside(NCH):
                        k = i - 1
                        wait(e, S("xc"), k)
                        wait(e, S("h0"), k - 2)
                        e.matmul(ps[k.off % 2][:, 0:CH], lin["nw0"][:, :], xc[k.off % 2], start=True, stop=True).then_inc(S("nw0"), 1)
                    if (i - 2).inside(NCH):
                        k = i - 2
                        wait(e, S("h0"), k)
                        wait(e, S("y"), k - 1)
                        e.matmul(ps[2][:, 0:CH], lin["fnw0"][:, :], Z0[:, cols(k)], start=True, stop=True).then_inc(S("fnw0"), 1)
                        wait(e, S("few_c"), k - 1)
                        e.matmul(ps[4][:, 0:CH], few0_h[:, :], Z0[:, cols(k)], start=True, stop=True).then_inc(S("few0"), 1)
                    if (i - 3).inside(NCH):
                        k = i - 3
                        wait(e, S("x1"), k)
                        wait(e, S("h1"), k - 1)
                        wait(e, S("h1c"), k - 1)
                        e.matmul(ps[5][:, 0:CH], nw1_pair[:, :], x1[k.off % 2], start=True, stop=True).then_inc(S("nw1"), 1)
                    if (i - 4).inside(NCH):
                        k = i - 4
                        b = k.off % 4
                        wait(e, S("h1c"), k)
                        wait(e, S("few_c"), k)
                        wait(e, S("rows"), k - 2)
                        for t in range(2):
                            at = slice(t * TILE, (t + 1) * TILE)
                            e.transpose(ps[6 + k.off % 2][0:TILE, t * ROW:t * ROW + D], few_c[b][:, at], ident[:, :])
                            ins = e.transpose(ps[6 + k.off % 2][0:TILE, t * ROW + D:(t + 1) * ROW], h1_c[b][:, at], ident[0:HALF, 0:HALF])
                        ins.then_inc(S("turn"), 1)
                pipeline(e, NCH, 4, 8, 4, step)

            def act(e, S):
                row_roots(e, S)

                def step(i):
                    if i.inside(NCH):
                        wait(e, S("n_turn"), i - 4)
                        normalized(e, mid_rows, i, nrow[i.off % 4]).then_inc(S("n"), 1)
                    if (i - 1).inside(NCH):
                        k = i - 1
                        wait(e, S("nw0"), k)
                        e.activation(Z0[HALF:P, cols(k)], ps[k.off % 2][HALF:P, 0:CH], ACT.Relu).then_inc(S("h0"), 1)
                    if (i - 2).inside(NCH):
                        k = i - 2
                        wait(e, S("fnw0"), k)
                        wait(e, S("nw1"), k - 2)
                        e.activation(x1[k.off % 2], ps[2][:, 0:CH], ACT.Relu, bias=bias(0, 0)).then_inc(S("y"), 1)
                    if (i - 3).inside(NCH):
                        k = i - 3
                        wait(e, S("nw1"), k)
                        e.activation(Z1[HALF:P, cols(k)], ps[5][HALF:P, 0:CH], ACT.Relu).then_inc(S("h1"), 1)
                    if (i - 4).inside(NCH):
                        k = i - 4
                        wait(e, S("turn"), k)
                        wait(e, S(TABLE[k.off % 4]), k, 4, -4 * (k.off % 4))
                        wait(e, S("high"), k - 4, 2)
                        e.activation(hrow[k.off % 4], ps[6 + k.off % 2][0:TILE, 0:2 * ROW].rearrange("p (k d) -> p k d", k=2),
                                     ACT.Copy).then_inc(S("rows"), 1)
                pipeline(e, NCH, 4, 8, 4, step)

            def dve(e, S):
                e.memset(zero, 0.0).then_inc(S("zero"), 1)
                row_scales(e, S)

                def step(i):
                    if i.inside(NCH):
                        wait(e, S("n_turn"), i)
                        wait(e, S("nw0"), i - 2)
                        e.tensor_copy(xc[i.off % 2], ps[3][:, 0:CH]).then_inc(S("xc"), 1)
                    if (i - 2).inside(NCH):
                        k = i - 2
                        wait(e, S("y"), k)
                        e.tensor_scalar(x1[k.off % 2], x1[k.off % 2], bias(0, 2), bias(0, 3), ALU.mult, ALU.add).then_inc(S("x1"), 1)
                        wait(e, S("few0"), k)
                        wait(e, S("turn"), k - 4)
                        e.tensor_copy(few_c[k.off % 4], ps[4][:, 0:CH]).then_inc(S("few_c"), 1)
                    if (i - 3).inside(NCH):
                        k = i - 3
                        wait(e, S("nw1"), k)
                        e.tensor_scalar(h1_c[k.off % 4], ps[5][0:HALF, 0:CH], 0.0, None, ALU.max).then_inc(S("h1c"), 1)
                    if (i - 5).inside(NCH):
                        k = i - 5
                        b = k.off % 4
                        wait(e, S("rows"), k)
                        wait(e, S(f"hp{b}"), k, 12, -12 * b)
                        e.tensor_copy(part[b][0], hrow[b]).then_inc(S("high"), 1)
                        wait(e, S("high"), k, 2, 1)
                        wait(e, S("low"), k - 2)
                        e.tensor_tensor(rest[b % 2], hrow[k.off % 4], part[b][0], ALU.subtract).then_inc(S("high"), 1)
                pipeline(e, NCH, 4, 12, 5, step)

            def pool(e, S):
                e.memset(Z1[0:HALF, :], 0.0).then_inc(S("z"), 1)
                e.memset(Z2[:, :], 0.0).then_inc(S("z"), 1)
                e.wait_ge(S("z"), 2)

                def step(i):
                    b = i.off % 4
                    wait(e, S("high"), i, 2)
                    wait(e, S(f"hp{b}"), i, 12, -12 * b)
                    begin(e, S)
                    e.tensor_copy(part[b][1], rest[b % 2]).then_inc(S("mid"), 1)
                    wait(e, S("mid"), i)
                    begin(e, S)
                    e.tensor_tensor(part[b][2], rest[b % 2], part[b][1], ALU.subtract).then_inc(S("low"), 1)
                pipeline(e, NCH, 4, 8, 0, step)

            def sync(e, S):
                e.dma_start(x_mid.rearrange("(t p) d -> p t d", p=TILE), mid_rows).then_inc(S("mid_out"), 16)
                e.wait_ge(S("zero"), 1)
                e.dma_start(h_parts[:, N:NP, :].rearrange("k r d -> r k d"),
                            zero.rearrange("r (k d) -> r k d", k=3)).then_inc(S("zeros"), 16)

                def step(i):
                    if i.inside(NCH):
                        wait(e, S("rows"), i)
                        begin(e, S)
                        e.dma_start(rows_of(h_table, i), hrow[i.off % 4]).then_inc(S(TABLE[i.off % 4]), 16)
                    if (i - 2).inside(NCH):
                        k = i - 2
                        b = k.off % 4
                        wait(e, S("low"), k)
                        begin(e, S)
                        for q in range(3):
                            e.dma_start(rows_of(h_parts[q, 0:N, :], k), part[b][q]).then_inc(S(f"hp{b}"), 16)
                pipeline(e, NCH, 4, 8, 2, step)
                stores(e, S, TABLE, NCH)
                for b in range(4):
                    e.wait_ge(S(f"hp{b}"), 48 * len(range(b, NCH, 4)))
                e.wait_ge(S("zeros"), 16)
                e.wait_ge(S("mid_out"), 16)

            names = "issued var root scale norm n n_turn xc mid_out nw0 fnw0 few0 nw1 turn h0 few_c y h1 h1c x1 rows high mid low zero zeros z hp0 hp1 hp2 hp3".split() + TABLE
            return ("hidden", names, dict(sync=sync, pool=pool, act=act, pe=pe, dve=dve))

        def edge_layers_phase():
            X1 = [xT_all[:, s * GE:(s + 1) * GE] for s in range(RING)]
            A, X2, C = ([work[:, 2 * n + b, :] for b in range(2)] for n in range(3))
            rows = ring[:, :, :, 0:ROW]
            left = xT_all[:, RING * GE:(RING + 1) * GE].rearrange("p (j c) -> p j c", j=J)
            parts = [[xT_all[:, (RING + 1) * GE + (3 * b + q) * GE // 2:(RING + 1) * GE + (3 * b + q + 1) * GE // 2]
                      .bitcast(BF16).rearrange("p (j c) -> p j c", j=J) for q in range(3)] for b in range(2)]
            onehot_b = onehot[:, :, :, :].rearrange("p s j w -> p (s j w)").bitcast(BF16).rearrange("p (s j w) -> p s j w", s=RING, j=J)
            TAG = "h"

            def sync(e, S):
                def step(i):
                    if i.inside(NG):
                        s = i.off % RING
                        wait(e, S("turn2"), i - RING)
                        begin(e, S)
                        wait(e, S("one_hotT"), i - 4)
                        begin(e, S)
                        at = bass.ds(i.times(1), 1)
                        src = rel_rows[at, :, :].rearrange("o j p -> o (j p)").broadcast_to([3 * W, GE])
                        e.dma_start(relb[:, i.off % 4, :], src).then_inc(S(f"rel{i.off % 4}"), 16)
                        w = e.value_load(starts[0:1, at], min_val=0, max_val=N - 1)
                        for q in range(3):
                            e.dma_start(window[q * W:(q + 1) * W, s, :], h_parts[q, bass.ds(w, W), :]).then_inc(S(f"window{s}"), 16)
                        e.dma_start(X1[s], e0_few[at, :, :].rearrange("o p q -> (o p) q")).then_inc(S(f"term{s}"), 16)
                pipeline(e, NG, RING, RING, 0, step)

            def pool(e, S):
                def step(i):
                    wait(e, S("turn2"), i - RING)
                    gathers(e, S, i, h_table, rows, TAG)
                pipeline(e, NG, RING, RING, 0, step)

            def turn(e, S, i, bank, c0, out_rows, w0):
                s = i.off % RING
                for j in range(J):
                    e.matmul(bank[:, j * P:(j + 1) * P], ring[:, s, j, c0:c0 + P], ident[:, :], is_transpose=True,
                             start=(j == 0), stop=False, skip_group_check=True)
                return e.matmul(bank[0:out_rows, :], window[:, s, w0:w0 + out_rows], onehotT[:, s % 4, :], start=False, stop=True,
                                skip_group_check=True)

            def pe(e, S):
                def step(i):
                    if i.inside(NG):
                        s = i.off % RING
                        gathered(e, S, i, TAG)
                        wait(e, S(f"window{s}"), i, 6, 48 - 6 * s)
                        wait(e, S("one_hotT"), i)
                        wait(e, S("X1"), i - 1)
                        turn(e, S, i, ps[0], 0, P, 0).then_inc(S("turn1"), 1)
                    if (i - 1).inside(NG):
                        k = i - 1
                        wait(e, S("A"), k)
                        wait(e, S("e1"), k - 2)
                        for j in range(J):
                            ins = e.matmul(ps[1 + k.off % 2][:, j * P:(j + 1) * P], A[k.off % 2][:, j * P:(j + 1) * P], ew1_pair[:, :],
                                           start=True, stop=True)
                        ins.then_inc(S("ew1"), 1)
                    if (i - 2).inside(NG):
                        k = i - 2
                        wait(e, S("e1"), k)
                        wait(e, S("X2"), k - 2)
                        turn(e, S, k, ps[3 + k.off % 2], D, HALF, D).then_inc(S("turn2"), 1)
                    if (i - 3).inside(NG):
                        k = i - 3
                        wait(e, S("X2"), k)
                        wait(e, S("C"), k - 1)
                        e.matmul(ps[5][:, :], lin["few1"][:, :], X2[k.off % 2], start=True, stop=True).then_inc(S("few1"), 1)
                    if (i - 4).inside(NG):
                        k = i - 4
                        wait(e, S("C"), k)
                        wait(e, S("e2"), k - 1)
                        for j in range(J):
                            ins = e.matmul(ps[6][:, j * P:(j + 1) * P], C[k.off % 2][:, j * P:(j + 1) * P], ew2_pair[:, :],
                                           start=True, stop=True)
                        ins.then_inc(S("ew2"), 1)
                    if (i - 7).inside(NG):
                        k = i - 7
                        s = k.off % RING
                        wait(e, S("low"), k)
                        wait(e, S("agg"), k - 1, 2)
                        wait(e, S("onehot"), k)
                        for j in range(J):
                            for q in range(3):
                                ins = e.matmul(ps[7][:, 0:W], parts[k.off % 2][q][:, j, :], onehot_b[:, s, j, 0:W],
                                               start=(j == q == 0), stop=(j == J - 1 and q == 2))
                        ins.then_inc(S("sums"), 1)
                pipeline(e, NG, RING, 2 * RING, 7, step)

            def act(e, S):
                first_indices(e, S)

                def by_edge(k, bank, c0, name):
                    return e.activation(ring[:, k.off % RING, :, c0:c0 + HALF],
                                        bank[:, :].rearrange("p (j c) -> p j c", j=J)[:, :, 0:HALF], ACT.Relu).then_inc(S(name), 1)

                def step(i):
                    if i.inside(NG):
                        gathered(e, S, i, TAG)
                        next_indices(e, S, i)
                        wait(e, S("X1"), i)
                        wait(e, S("ew1"), i - 2)
                        e.activation(A[i.off % 2], X1[i.off % RING], ACT.Relu, bias=bias(0, 1)).then_inc(S("A"), 1)
                    if (i - 1).inside(NG):
                        wait(e, S("ew1"), i - 1)
                        by_edge(i - 1, ps[1 + (i.off - 1) % 2], ROW, "e1")
                    if (i - 6).inside(NG):
                        k = i - 6
                        wait(e, S("left"), k)
                        e.activation(parts[k.off % 2][1], left, ACT.Copy).then_inc(S("mid"), 1)
                    if (i - 5).inside(NG):
                        k = i - 5
                        wait(e, S("e2"), k)
                        wait(e, S("sums"), k - 2)
                        e.activation(parts[k.off % 2][0], ring[:, k.off % RING, :, ROW:ROW + D], ACT.Copy).then_inc(S("high"), 1)
                    if (i - 3).inside(NG):
                        k = i - 3
                        wait(e, S("few1"), k)
                        wait(e, S("ew2"), k - 2)
                        e.activation(C[k.off % 2], ps[5][:, :], ACT.Relu, bias=bias(1, 1)).then_inc(S("C"), 1)
                    if (i - 4).inside(NG):
                        wait(e, S("ew2"), i - 4)
                        by_edge(i - 4, ps[6], ROW + HALF, "e2")
                pipeline(e, NG, RING, RING, 6, step)

            def dve(e, S):
                def hots(i):
                    wait(e, S(f"rel{i.off % 4}"), i, 4, 16 - 4 * (i.off % 4))
                    wait(e, S("turn2"), i - 4)
                    e.tensor_scalar(onehotT[:, i.off % 4, :], relb[:, i.off % 4, :], iota_p[0:3 * W, :], None,
                                    ALU.is_equal).then_inc(S("one_hotT"), 1)

                def step(i):
                    if i.base is None and i.off == 0:
                        hots(i)
                    if (i - -1).inside(NG):
                        hots(i - -1)
                    if i.inside(NG):
                        s = i.off % RING
                        wait(e, S("turn1"), i)
                        wait(e, S(f"term{s}"), i, 2, 16 - 2 * s)
                        e.tensor_tensor(X1[s], X1[s], ps[0][:, :], ALU.add).then_inc(S("X1"), 1)
                    if (i - 2).inside(NG):
                        k = i - 2
                        wait(e, S("turn2"), k)
                        wait(e, S("few1"), k - 2)
                        e.tensor_copy(X2[k.off % 2], ps[3 + k.off % 2][:, :]).then_inc(S("X2"), 1)
                    if (i - 8).inside(NG):
                        k = i - 8
                        w = window_start(e, k)
                        wait(e, S("sums"), k)
                        wait(e, S("agg"), k - 1, 2)
                        for half, Z in ((slice(0, HALF), Z1), (slice(HALF, P), Z2)):
                            place = Z[half, bass.ds(w, W)]
                            e.tensor_tensor(place, place, ps[7][half, 0:W], ALU.add).then_inc(S("agg"), 1)
                    if (i - 4).inside(NG):
                        k = i - 4
                        wait(e, S("sums"), k - RING)
                        make_onehot(e, k, onehot_b).then_inc(S("onehot"), 1)
                    if (i - 6).inside(NG):
                        k = i - 6
                        wait(e, S("mid"), k)
                        e.tensor_tensor(parts[k.off % 2][2], left, parts[k.off % 2][1], ALU.subtract).then_inc(S("low"), 1)
                    if (i - 5).inside(NG):
                        k = i - 5
                        wait(e, S("high"), k)
                        wait(e, S("low"), k - 1)
                        e.tensor_tensor(left, ring[:, k.off % RING, :, ROW:ROW + D], parts[k.off % 2][0],
                                        ALU.subtract).then_inc(S("left"), 1)
                pipeline(e, NG, RING, 2 * RING, 8, step)

            names = ["issued", "idx", "high", "left", "mid", "low", "sums", "one_hotT", "onehot", "X1", "X2", "turn1", "turn2", "few1", "A", "C",
                     "ew1", "ew2", "e1", "e2", "agg"] + [f"{n}{s}" for n in ("window", "term") for s in range(RING)] + \
                    [f"rel{s}" for s in range(4)]
            return ("edge layers", names + ALL,
                    either(1, edge_layers_general(), dict(sync=sync, pool=pool, act=act, pe=pe, dve=dve)))

        def output_phase():
            y = [work[:, b, 0:CH] for b in range(2)]
            z = [work[:, b, 256:256 + CH] for b in range(2)]
            xm = rowring(2)
            orow = rowring(4)
            MID = ["mid0", "mid1", "mid2", "mid3"]

            def pe(e, S):
                def step(i):
                    if i.inside(NCH):
                        wait(e, S("y"), i - 2)
                        e.matmul(ps[i.off % 2][:, 0:CH], lin["fnw1"][:, :], Z1[:, cols(i)], start=True, stop=True).then_inc(S("fnw1"), 1)
                    if (i - 1).inside(NCH):
                        k = i - 1
                        wait(e, S("x2"), k)
                        wait(e, S("h2"), k - 2)
                        e.matmul(ps[2 + k.off % 2][0:HALF, 0:CH], lin["nw2"][:, :], y[k.off % 2], start=True, stop=True).then_inc(S("nw2"), 1)
                    if (i - 2).inside(NCH):
                        k = i - 2
                        wait(e, S("h2"), k)
                        wait(e, S("z"), k - 2)
                        e.matmul(ps[4 + k.off % 2][:, 0:CH], lin["fnw2"][:, :], Z2[:, cols(k)], start=True, stop=True).then_inc(S("fnw2"), 1)
                    if (i - 3).inside(NCH):
                        k = i - 3
                        wait(e, S("x3"), k)
                        wait(e, S("out"), k - 2)
                        for t in range(2):
                            ins = e.transpose(ps[6 + k.off % 2][0:TILE, t * D:(t + 1) * D], z[k.off % 2][:, t * TILE:(t + 1) * TILE],
                                              ident[:, :])
                        ins.then_inc(S("turn"), 1)
                pipeline(e, NCH, 4, 8, 3, step)

            def act(e, S):
                def step(i):
                    if i.inside(NCH):
                        wait(e, S("fnw1"), i)
                        wait(e, S("nw2"), i - 2)
                        e.activation(y[i.off % 2], ps[i.off % 2][:, 0:CH], ACT.Relu, bias=bias(1, 0)).then_inc(S("y"), 1)
                    if (i - 1).inside(NCH):
                        k = i - 1
                        wait(e, S("nw2"), k)
                        e.activation(Z2[0:HALF, cols(k)], ps[2 + k.off % 2][0:HALF, 0:CH], ACT.Relu).then_inc(S("h2"), 1)
                    if (i - 2).inside(NCH):
                        k = i - 2
                        wait(e, S("fnw2"), k)
                        wait(e, S("turn"), k - 2)
                        e.activation(z[k.off % 2], ps[4 + k.off % 2][:, 0:CH], ACT.Relu, bias=bias(2, 0)).then_inc(S("z"), 1)
                pipeline(e, NCH, 4, 4, 2, step)

            def dve(e, S):
                def step(i):
                    if i.inside(NCH):
                        wait(e, S("y"), i)
                        e.tensor_scalar(y[i.off % 2], y[i.off % 2], bias(1, 2), bias(1, 3), ALU.mult, ALU.add).then_inc(S("x2"), 1)
                    if (i - 2).inside(NCH):
                        k = i - 2
                        wait(e, S("z"), k)
                        e.tensor_scalar(z[k.off % 2], z[k.off % 2], bias(2, 2), bias(2, 3), ALU.mult, ALU.add).then_inc(S("x3"), 1)
                    if (i - 3).inside(NCH):
                        k = i - 3
                        b = k.off % 4
                        wait(e, S("turn"), k)
                        wait(e, S(MID[b]), k, 4, 16 - 4 * b)
                        wait(e, S(TABLE[b]), k, 4, -4 * b)
                        e.tensor_tensor(orow[b], xm[b], ps[6 + k.off % 2][0:TILE, 0:2 * D].rearrange("p (k d) -> p k d", k=2),
                                        ALU.add).then_inc(S("out"), 1)
                pipeline(e, NCH, 4, 8, 3, step)

            def sync(e, S):
                def step(i):
                    if i.inside(NCH):
                        wait(e, S("out"), i - 4)
                        begin(e, S)
                        e.dma_start(xm[i.off % 4], rows_of(x_mid, i)).then_inc(S(MID[i.off % 4]), 16)
                    if (i - 4).inside(NCH):
                        k = i - 4
                        wait(e, S("out"), k)
                        begin(e, S)
                        e.dma_start(rows_of(out, k), orow[k.off % 4]).then_inc(S(TABLE[k.off % 4]), 16)
                pipeline(e, NCH, 4, 4, 4, step)
                stores(e, S, TABLE, NCH)

            names = "issued fnw1 nw2 fnw2 turn y h2 z x2 x3 out".split() + TABLE + MID
            return ("output", names, dict(sync=sync, act=act, pe=pe, dve=dve))

        phases += [hidden_phase(), edge_layers_phase(), output_phase()]

        bar = sem("bar")
        shared = [sem(f"phase_sem{k}") for k in range(max(len(used) for _, used, _ in phases))]
        gather_sems = {}

        def names_of(used):
            def S(name):
                if name.startswith("gather"):
                    if name not in gather_sems:
                        gather_sems[name] = sem(name)
                    return gather_sems[name]
                return shared[used.index(name)]
            return S

        block = ctx.enter_context(nc.Block())

        def program(e, who):
            met = [0]

            def meet():
                met[0] += 1
                e.drain()
                e.sem_inc(bar, 1)
                e.wait_ge(bar, 5 * met[0])
                e.drain()

            for name, used, parts in phases:
                S = names_of(used)
                if who in parts:
                    parts[who](e, S)
                meet()
                if who == "sync":
                    for n in used:
                        e.sem_clear(S(n))
                meet()

        @block.sync
        def _(e):
            program(e, "sync")

        @block.gpsimd
        def _(e):
            program(e, "pool")

        @block.scalar
        def _(e):
            program(e, "act")

        @block.tensor
        def _(e):
            program(e, "pe")

        @block.vector
        def _(e):
            program(e, "dve")


_OUT = (N, D)


def kernel(**inputs):
    import numpy as np
    import concourse.bacc as bacc
    from concourse.bass_utils import run_bass_kernel_spmd
    nc = bacc.Bacc("TRN2", target_bir_lowering=False, num_devices=1)
    arrays, a = {}, {}
    for name, v in inputs.items():
        v = np.ascontiguousarray(v)
        arrays["in_" + name] = v
        a[name] = nc.dram_tensor("in_" + name, v.shape, mybir.dt.from_np(v.dtype), kind="ExternalInput").ap()
    out = nc.dram_tensor("out_nodes", _OUT, F32, kind="ExternalOutput").ap()
    gnn_kernel(nc, a, out)
    r = run_bass_kernel_spmd(nc, [arrays], core_ids=[0])
    return r.results[0]["out_nodes"]
```
